# Optimizing a Trainium2 kernel written in Bass

```python
import numpy as np
import jax
import jax.numpy as jnp

def _softmax(x, axis=-1):
    return jax.nn.softmax(x, axis=axis)

def _gelu(x):
    return jax.nn.gelu(x, approximate=True)

def _silu(x):
    return jax.nn.silu(x)

def _sigmoid(x):
    return jax.nn.sigmoid(x)

def _layernorm(x, axis=-1, eps=1e-05):
    m = jnp.mean(x, axis=axis, keepdims=True)
    v = jnp.var(x, axis=axis, keepdims=True)
    return (x - m) / jnp.sqrt(v + eps)

def _scatter_add(tgt, idx, src, axis=0):
    return tgt.at[idx].add(src)

def _segment_sum(src, seg, n):
    return jax.ops.segment_sum(src, seg, n)
kernel_name = 'mk_decoder_postln_d1_seqx_r8_bb650a'

def setup_inputs(seed: int=0):
    np.random.seed(seed)
    _w = jnp.asarray

    def _rec_inputs():
        import jax
        import jax.numpy as jnp
        _rk = jax.random.key(seed)
        x = -0.0002928 + 1 * jax.random.normal(jax.random.fold_in(_rk, 1), (16, 64, 256), jnp.float32)
        _lenS = 64 - jax.random.randint(jax.random.fold_in(_rk, 7), (16,), 0, max(1, 64 // 4) + 1, jnp.int32)
        _lenS2 = 64 - jax.random.randint(jax.random.fold_in(_rk, 8), (16,), 0, max(1, 64 // 4) + 1, jnp.int32)
        _ctx_2048P = jax.random.normal(jax.random.fold_in(_rk, 11), (16, 16, 256), jnp.float32)
        _ctx_2048c = jax.random.dirichlet(jax.random.fold_in(_rk, 511), 0.3 * jnp.ones((16,), jnp.float32), (16, 64))
        _ctx_2048t = jnp.einsum('bsk,bkd->bsd', _ctx_2048c, _ctx_2048P)
        _ctx_2048t = _ctx_2048t * jax.lax.rsqrt(jnp.mean(jnp.square(_ctx_2048t)) + 1e-12) * 0.953939
        ctx_2048 = 4.13588e-05 + 0.999923 * (_ctx_2048t + 0.3 * jax.random.normal(jax.random.fold_in(_rk, 611), (16, 64, 256), jnp.float32))
        _validS = jnp.arange(64)[None, :] < _lenS[:, None]
        _validS2 = jnp.arange(64)[None, :] < _lenS2[:, None]
        _causal = jnp.tril(jnp.ones((64, 64), dtype=bool))
        mask_1xSxS2_ff0 = jnp.where(jnp.ones((1, 64, 64), dtype=bool), 0.0, -1000000000.0).astype(jnp.float32)
        return (x, ctx_2048, mask_1xSxS2_ff0)
    x, ctx_2048, mask_1xSxS2_ff0 = _rec_inputs()

    def _L0_attn_setup():
        import jax, jax.numpy as jnp
        import numpy as np
        import math
        D_MODEL = 256
        NUM_HEADS = 16
        HEAD_DIM = D_MODEL // NUM_HEADS
        key = jax.random.key(seed)
        k_x, k_wqkv, k_bqkv, k_wo, k_bo = jax.random.split(key, 5)
        B, S = (2, 256)
        scale = 1.0 / math.sqrt(D_MODEL)
        return {'x': jax.random.normal(k_x, (B, S, D_MODEL), dtype=jnp.float32), 'w_qkv': jax.random.normal(k_wqkv, (3 * D_MODEL, D_MODEL), dtype=jnp.float32) * scale, 'b_qkv': jax.random.normal(k_bqkv, (3 * D_MODEL,), dtype=jnp.float32) * 0.01, 'w_out': jax.random.normal(k_wo, (D_MODEL, D_MODEL), dtype=jnp.float32) * scale, 'b_out': jax.random.normal(k_bo, (D_MODEL,), dtype=jnp.float32) * 0.01}
    _L0_attn_all = _L0_attn_setup()
    _L0_attn_in = {k: v for k, v in _L0_attn_all.items() if k in ('w_qkv', 'b_qkv', 'w_out', 'b_out')}
    del _L0_attn_all

    def _L0_xattn_setup():
        import jax, jax.numpy as jnp
        import numpy as np
        H = 256
        NH = 16
        NKV = 4
        HD = 128
        GROUPS = NH // NKV
        EPS = 1e-06
        B, S, SE = (1, 256, 512)

        def _rmsnorm(x, w, eps=EPS):
            xf = x.astype(jnp.float32)
            var = jnp.mean(xf * xf, axis=-1, keepdims=True)
            return (xf * jax.lax.rsqrt(var + eps)).astype(x.dtype) * w
        key = jax.random.key(seed)
        ks = jax.random.split(key, 12)
        sc = 0.02
        return {'hidden_states': jax.random.normal(ks[0], (B, S, H), jnp.float32), 'encoder_hidden_states': jax.random.normal(ks[1], (B, SE, H), jnp.float32), 'attention_mask': jnp.zeros((B, S, SE), jnp.float32), 'Wq': jax.random.normal(ks[2], (H, NH * HD), jnp.float32) * sc, 'bq': jax.random.normal(ks[3], (NH * HD,), jnp.float32) * sc, 'Wk': jax.random.normal(ks[4], (H, NKV * HD), jnp.float32) * sc, 'bk': jax.random.normal(ks[5], (NKV * HD,), jnp.float32) * sc, 'Wv': jax.random.normal(ks[6], (H, NKV * HD), jnp.float32) * sc, 'bv': jax.random.normal(ks[7], (NKV * HD,), jnp.float32) * sc, 'Wo': jax.random.normal(ks[8], (NH * HD, H), jnp.float32) * sc, 'qn_w': jnp.ones((HD,), jnp.float32), 'kn_w': jnp.ones((HD,), jnp.float32)}
    _L0_xattn_all = _L0_xattn_setup()
    _L0_xattn_in = {k: v for k, v in _L0_xattn_all.items() if k in ('Wq', 'bq', 'Wk', 'bk', 'Wv', 'bv', 'Wo', 'qn_w', 'kn_w')}
    del _L0_xattn_all

    def _L0_ffn_setup():
        import jax, jax.numpy as jnp
        import numpy as np
        H = 256
        key = jax.random.key(seed)
        ks = jax.random.split(key, 10)
        s = 1.0 / np.sqrt(H)
        x = jax.random.normal(ks[0], (4, 256, H), dtype=jnp.float32)
        Wg = jax.random.uniform(ks[1], (2, H), jnp.float32, -s, s)
        W0a = jax.random.uniform(ks[2], (2 * H, H), jnp.float32, -s, s)
        b0a = jax.random.uniform(ks[3], (2 * H,), jnp.float32, -s, s)
        W0b = jax.random.uniform(ks[4], (H, 2 * H), jnp.float32, -s, s)
        b0b = jax.random.uniform(ks[5], (H,), jnp.float32, -s, s)
        W1a = jax.random.uniform(ks[6], (2 * H, H), jnp.float32, -s, s)
        b1a = jax.random.uniform(ks[7], (2 * H,), jnp.float32, -s, s)
        W1b = jax.random.uniform(ks[8], (H, 2 * H), jnp.float32, -s, s)
        b1b = jax.random.uniform(ks[9], (H,), jnp.float32, -s, s)
        return {'x': x, 'Wg': Wg, 'W0a': W0a, 'b0a': b0a, 'W0b': W0b, 'b0b': b0b, 'W1a': W1a, 'b1a': b1a, 'W1b': W1b, 'b1b': b1b}
    _L0_ffn_all = _L0_ffn_setup()
    _L0_ffn_in = {k: v for k, v in _L0_ffn_all.items() if k in ('Wg', 'W0a', 'b0a', 'W0b', 'b0b', 'W1a', 'b1a', 'W1b', 'b1b')}
    del _L0_ffn_all
    return {'x': x, 'ctx_2048': ctx_2048, 'mask_1xSxS2_ff0': mask_1xSxS2_ff0, 'L0_attn_w_qkv': _L0_attn_in['w_qkv'], 'L0_attn_b_qkv': _L0_attn_in['b_qkv'], 'L0_attn_w_out': _L0_attn_in['w_out'], 'L0_attn_b_out': _L0_attn_in['b_out'], 'L0_xattn_Wq': _L0_xattn_in['Wq'], 'L0_xattn_bq': _L0_xattn_in['bq'], 'L0_xattn_Wk': _L0_xattn_in['Wk'], 'L0_xattn_bk': _L0_xattn_in['bk'], 'L0_xattn_Wv': _L0_xattn_in['Wv'], 'L0_xattn_bv': _L0_xattn_in['bv'], 'L0_xattn_Wo': _L0_xattn_in['Wo'], 'L0_xattn_qn_w': _L0_xattn_in['qn_w'], 'L0_xattn_kn_w': _L0_xattn_in['kn_w'], 'L0_ffn_Wg': _L0_ffn_in['Wg'], 'L0_ffn_W0a': _L0_ffn_in['W0a'], 'L0_ffn_b0a': _L0_ffn_in['b0a'], 'L0_ffn_W0b': _L0_ffn_in['W0b'], 'L0_ffn_b0b': _L0_ffn_in['b0b'], 'L0_ffn_W1a': _L0_ffn_in['W1a'], 'L0_ffn_b1a': _L0_ffn_in['b1a'], 'L0_ffn_W1b': _L0_ffn_in['W1b'], 'L0_ffn_b1b': _L0_ffn_in['b1b']}

def reference(x, ctx_2048, mask_1xSxS2_ff0, L0_attn_w_qkv, L0_attn_b_qkv, L0_attn_w_out, L0_attn_b_out, L0_xattn_Wq, L0_xattn_bq, L0_xattn_Wk, L0_xattn_bk, L0_xattn_Wv, L0_xattn_bv, L0_xattn_Wo, L0_xattn_qn_w, L0_xattn_kn_w, L0_ffn_Wg, L0_ffn_W0a, L0_ffn_b0a, L0_ffn_W0b, L0_ffn_b0b, L0_ffn_W1a, L0_ffn_b1a, L0_ffn_W1b, L0_ffn_b1b):
    import jax
    import jax.numpy as jnp

    def _L0_attn_ref(x, w_qkv, b_qkv, w_out, b_out):
        import jax, jax.numpy as jnp
        import numpy as np
        import math
        D_MODEL = 256
        NUM_HEADS = 16
        HEAD_DIM = D_MODEL // NUM_HEADS
        B, S, D = x.shape
        H, Hd = (NUM_HEADS, HEAD_DIM)
        qkv = jnp.einsum('bsd,ed->bse', x, w_qkv) + b_qkv
        qkv = qkv.reshape(B, S, 3, H, Hd)
        q = jnp.transpose(qkv[:, :, 0], (0, 2, 1, 3))
        k = jnp.transpose(qkv[:, :, 1], (0, 2, 1, 3))
        v = jnp.transpose(qkv[:, :, 2], (0, 2, 1, 3))
        scores = jnp.einsum('bhqd,bhkd->bhqk', q, k) / math.sqrt(Hd)
        causal = jnp.triu(jnp.full((S, S), -jnp.inf, dtype=scores.dtype), k=1)
        scores = scores + causal[None, None]
        attn = jax.nn.softmax(scores, axis=-1)
        out = jnp.einsum('bhqk,bhkd->bhqd', attn, v)
        out = jnp.transpose(out, (0, 2, 1, 3)).reshape(B, S, D)
        return jnp.einsum('bsd,ed->bse', out, w_out) + b_out

    def _L0_xattn_ref(hidden_states, encoder_hidden_states, attention_mask, Wq, bq, Wk, bk, Wv, bv, Wo, qn_w, kn_w):
        import jax, jax.numpy as jnp
        import numpy as np
        H = 256
        NH = 16
        NKV = 4
        HD = 128
        GROUPS = NH // NKV
        EPS = 1e-06
        B, S, SE = (1, 256, 512)

        def _rmsnorm(x, w, eps=EPS):
            xf = x.astype(jnp.float32)
            var = jnp.mean(xf * xf, axis=-1, keepdims=True)
            return (xf * jax.lax.rsqrt(var + eps)).astype(x.dtype) * w
        b, s, _ = hidden_states.shape
        se = encoder_hidden_states.shape[1]
        q = (hidden_states @ Wq + bq).reshape(b, s, NH, HD).transpose(0, 2, 1, 3)
        k = (encoder_hidden_states @ Wk + bk).reshape(b, se, NKV, HD).transpose(0, 2, 1, 3)
        v = (encoder_hidden_states @ Wv + bv).reshape(b, se, NKV, HD).transpose(0, 2, 1, 3)
        k = jnp.repeat(k, GROUPS, axis=1)
        v = jnp.repeat(v, GROUPS, axis=1)
        q = _rmsnorm(q, qn_w)
        k = _rmsnorm(k, kn_w)
        scale = 1.0 / np.sqrt(HD).astype(np.float32)
        scores = jnp.einsum('bhsd,bhed->bhse', q, k) * scale
        scores = scores + attention_mask[:, None, :, :]
        probs = jax.nn.softmax(scores.astype(jnp.float32), axis=-1).astype(q.dtype)
        out = jnp.einsum('bhse,bhed->bhsd', probs, v)
        out = out.transpose(0, 2, 1, 3).reshape(b, s, NH * HD)
        return out @ Wo

    def _L0_ffn_ref(x, Wg, W0a, b0a, W0b, b0b, W1a, b1a, W1b, b1b):
        import jax, jax.numpy as jnp
        import numpy as np
        H = 256
        scores = jax.nn.softmax(jnp.einsum('bsh,eh->bse', x, Wg), axis=-1)
        top_expert = jnp.argmax(scores, axis=-1)
        h0 = jax.nn.gelu(jnp.einsum('bsh,fh->bsf', x, W0a) + b0a, approximate=False)
        out0 = jnp.einsum('bsf,hf->bsh', h0, W0b) + b0b
        h1 = jax.nn.relu(jnp.einsum('bsh,fh->bsf', x, W1a) + b1a)
        out1 = jnp.einsum('bsf,hf->bsh', h1, W1b) + b1b
        mask0 = (top_expert == 0).astype(x.dtype)[..., None]
        return out0 * mask0 + out1 * (1.0 - mask0)
    x = _layernorm(x + _L0_attn_ref(x, L0_attn_w_qkv, L0_attn_b_qkv, L0_attn_w_out, L0_attn_b_out), axis=-1)
    x = _layernorm(x + _L0_xattn_ref(x, ctx_2048, mask_1xSxS2_ff0, L0_xattn_Wq, L0_xattn_bq, L0_xattn_Wk, L0_xattn_bk, L0_xattn_Wv, L0_xattn_bv, L0_xattn_Wo, L0_xattn_qn_w, L0_xattn_kn_w), axis=-1)
    x = _layernorm(x + _L0_ffn_ref(x, L0_ffn_Wg, L0_ffn_W0a, L0_ffn_b0a, L0_ffn_W0b, L0_ffn_b0b, L0_ffn_W1a, L0_ffn_b1a, L0_ffn_W1b, L0_ffn_b1b), axis=-1)
    return x

_drawn_inputs = setup_inputs


def setup_inputs(seed=0):
    import zlib

    import numpy as np

    out = dict(_drawn_inputs(seed))
    spreads = {'L0_xattn_qn_w': (1.0, 0.2), 'L0_xattn_kn_w': (1.0, 0.6)}
    factors = {'L0_attn_b_out': 3.548,
     'L0_xattn_bq': 2.922,
     'L0_xattn_bk': 6.086,
     'L0_ffn_b0a': 4.712,
     'L0_ffn_b1a': 4.249}
    for name, (base, spread) in spreads.items():
        noise = np.random.default_rng([zlib.crc32(name.encode()), seed]).standard_normal(out[name].shape)
        drawn = base * np.exp(spread * noise) if base else spread * noise
        out[name] = jnp.asarray(drawn.astype(out[name].dtype))
    for name, factor in factors.items():
        out[name] = (out[name] * factor).astype(out[name].dtype)
    return out
```

```python
import concourse.bass as bass
from concourse import mybir
from contextlib import ExitStack

D = 256
NB, S = 16, 64
TOK = NB * S
T = 256
NT = TOK // T
NC = TOK // 128
KC = D // 128
SH, SD = 16, 16
XH, XKV, XD = 16, 4, 128
GH = XH // XKV
NX = XKV * NT
NA = NT * 4
FF = 512
FC = FF // 128
NBANK = 7
NSTAGE = 2
SLOT = 1024
SPLITS = ((0, 0), (0, 1), (1, 0))
LN_EPS, RMS_EPS = 1e-5, 1e-6
HIDDEN = -1.0e30

C_BQ, C_BUP, C_QN, C_KN, C_HEAD, C_SECOND, NCOLS = 0, 16, 24, 25, 26, 28, 29
RW = 768
R_QKV, R_OUT, R_K, R_V, R_DOWN = (0, 0), (1, 512), (1, 0), (2, 0), ((2, 512), (3, 0))

ITEMS = ([("x", 0), ("qk", 0), ("v", 0), ("ctx", 0), ("wk", 0), ("wv", 0), ("aout", 0)]
         + [("x", 1), ("ctx", 1), ("x", 2), ("ctx", 2), ("x", 3), ("ctx", 3)]
         + [("xq", 0), ("xo", 0), ("xq", 1), ("xo", 1)]
         + [("up", 0), ("up", 1), ("down", 0), ("down", 1)]
         + [("xq", 2), ("xo", 2), ("xq", 3), ("xo", 3)])
LOW_ON_POOL = [i % 2 == 1 and i > 6 for i in range(len(ITEMS))]


def block_of(b, i):
    return (b % 2) * 4 + (b // 2) * 2 + i


def schedule():
    out, items = [], iter(range(len(ITEMS)))

    def load(n=1):
        out.extend(("load", next(items)) for _ in range(n))

    load(3)
    out.append(("a_project", 0))
    load(3)
    out.append(("v_copies", 0))
    loads = {0: 2, 2: 1, 4: 1, 5: 1, 8: 1, 9: 1, 11: 1, 12: 1, 13: 1, 14: 1}
    for n in range(NA + 3):
        if n < NA:
            out += [("a_scores", n), ("soft_a", n)]
            if n % 4 == 3 and n // 4 + 1 < NT:
                out.append(("a_project", n // 4 + 1))
        if 1 <= n <= NA:
            out.append(("soft_b", n - 1))
        if n < NA:
            out.append(("soft_m", n))
        if n % 2 == 0 and n // 2 <= NC:
            if n:
                out.append(("k_turn", n // 2 - 1))
            if n // 2 < NC:
                out.append(("kv_project", n // 2))
        if 1 <= n <= NA:
            out.append(("soft_c", n - 1))
        load(loads.get(n, 0))
        if 2 <= n < NA + 2:
            out.append(("turn", n - 2))
        if n >= 3:
            m, t = n - 3, (n - 3) // 4
            out.append(("a_values", m))
            if m % 4 == 3:
                out.append(("a_split", t))
                if t + 1 < NT:
                    out.append(("v_copies", t + 1))
                out += [("a_out", t), ("norm", (0, t))]
            if m % 4 == 0 and t:
                out.append(("norm_end", (0, t - 1)))
            if m % 4 == 1 and t:
                out.append(("norm_turn", (0, t - 1)))
    out += [("norm_end", (0, NT - 1)), ("x_query", 0), ("x_squares", 0), ("norm_turn", (0, NT - 1))]
    loads = {1: 1, 2: 1, 3: 1, 4: 1, 5: 1, 7: 1, 8: 1, 11: 1}
    for s in range(NX + 4):
        if s < NX:
            out.append(("x_scores", s))
        if 1 <= s <= NX:
            out.append(("soft_b", NA + s - 1))
        if s < NX:
            out.append(("soft_a", NA + s))
        if s + 1 < NX:
            out.append(("x_query", s + 1))
        if s < NX:
            out.append(("soft_m", NA + s))
        if 1 <= s <= NX:
            out.append(("soft_c", NA + s - 1))
        load(loads.get(s, 0))
        if 1 <= s <= NX:
            out.append(("turn", NA + s - 1))
        if s + 1 < NX:
            out.append(("x_squares", s + 1))
        if 3 <= s <= NX + 2:
            out.append(("x_out", s - 3))
            if s - 3 >= NX - NT:
                out.append(("norm", (1, (s - 3) % NT)))
        if 2 <= s <= NX + 1:
            out.append(("x_values", s - 2))
        if NX - NT <= s - 3 < NX:
            out.append(("norm_end", (1, (s - 3) % NT)))
        if s - 4 >= NX - NT:
            t = (s - 4) % NT
            out += [("norm_turn", (1, t)), ("gate", t)]
            out += [("f_up", (t, 0, 0)), ("f_up", (t, 0, 1)), ("f_up", (t, 1, 0)), ("f_down", (t, 0))]
            out += [("f_up", (t, 1, 1)), ("f_down", (t, 1))]
            out += [("norm", (2, t)), ("norm_end", (2, t)), ("store", t)]
    assert next(items, None) is None
    return out


STAGE_JOBS = {
    "a_project": ("dve",) * 3, "a_scores": ("dve",), "turn": ("act",), "a_out": ("dve",),
    "norm_turn": ("dve",), "kv_project": ("dve",) * 2, "k_turn": ("dve",), "x_query": ("dve",) * 2,
    "x_squares": ("dve",), "x_scores": ("dve",), "x_values": ("dve",) * 2, "x_out": ("dve",),
    "f_up": ("act",), "f_down": ("dve",),
}
SCHEDULE = schedule()


def number_jobs():
    first, engines = {}, []
    for name, k in SCHEDULE:
        jobs = STAGE_JOBS.get(name, ())
        if jobs:
            first[name, k] = len(engines)
            engines += jobs
    ends, count = {}, {"dve": 0, "act": 0}
    for name, k in SCHEDULE:
        if name == "soft_a":
            jobs = [first["a_scores", k] if k < NA else first["x_scores", k - NA]]
        elif name in ("a_scores", "x_scores"):
            jobs = []
        else:
            jobs = [first[name, k] + i for i in range(len(STAGE_JOBS.get(name, ())))]
        for job in jobs:
            count[engines[job]] += 1
            ends[job] = (engines[job], count[engines[job]])
    return first, ends


FIRST_JOB, JOB_ENDS = number_jobs()


def decoder(nc, xT, x, ctxT, wqkvT, woutT, Wq, Wk, Wv, Wo, WupT, WdownT, bias_rows, columns, gate_w, mask,
            causal, identity, out):
    f32, f32r, f16, bf16 = mybir.dt.float32, mybir.dt.float32r, mybir.dt.float16, mybir.dt.bfloat16
    ALU, ACT, AX = mybir.AluOpType, mybir.ActivationFunctionType, mybir.AxisListType

    ctx = ExitStack()
    with ctx:
        def sb(name, shape, dt):
            return ctx.enter_context(nc.sbuf_tensor(name, shape, dt))

        def sem(name):
            return ctx.enter_context(nc.semaphore(name))

        stage = sb("stage", [128, NSTAGE, SLOT], f32)
        acts = sb("acts", [128, 2, KC, TOK], f32r)
        resid = sb("resid", [128, NC, D], f32)
        w_kv = sb("w_kv", [128, 2, 2, 1024], f32r)
        w_a = sb("w_a", [128, 4096], f32r)
        w_xq = sb("w_xq", [128, 2, 2, 1024], f32r)
        w_xo = sb("w_xo", [128, 2, 2, 1024], f32r)
        parts = sb("parts", [128, 2, 1024], f32r)
        rows = sb("rows", [128, RW], f32r)
        ones = sb("ones", [128, T], f32r)
        keys = sb("keys", [128, 2, XKV, TOK], f16)
        values = sb("values", [128, NB, 2, XKV * XD], f16)
        queries = sb("queries", [128, 2, 2, 1024], f16)
        a_values_sb = queries[:, :, :, :].rearrange("p a b c -> p (a b c)")\
            .rearrange("p (b l n) -> p b l n", b=4, l=2)
        a_q = sb("a_q", [128, 2, 8, 128], f16)
        a_k = sb("a_k", [128, 2, 512], f16)
        v_spread = sb("v_spread", [128, 2, 2, 512], f16)
        v_parts = sb("v_parts", [128, 2, 512], f16)
        k_raw = sb("k_raw", [128, 512], f32)
        k_sq = sb("k_sq", [128, 512], f32)
        sq = v_spread[:, :, :, :].rearrange("p j l n -> p (j l n)").bitcast(f32)
        sq_hi = a_q[:, 0, :, :].rearrange("p e n -> p (e n)").bitcast(bf16)
        sq_lo = a_q[:, 1, :, :].rearrange("p e n -> p (e n)")
        scores = sb("scores", [128, 2, 512], f32)
        probs = sb("probs", [128, 2, 8, 128], f16)
        probsT = sb("probsT", [128, 2, 8, 128], f16)
        attn = sb("attn", [128, 2, 1024], f32r)
        hidden = k_sq, k_raw
        cols = sb("cols", [128, NCOLS], f32)
        key_scale = sb("key_scale", [128, 1], f32)
        gate_sb = sb("gate_sb", [128, 2, D], f32)
        gate_junk = sb("gate_junk", [128, D], bf16)
        logits = sb("logits", [128, 2, 2], f32)
        routed = sb("routed", [128, 2, 2], f32)
        mask_sb = sb("mask_sb", [128, S], f32)
        causal_sb = sb("causal_sb", [128, S], f32)
        ident = sb("ident", [128, 128], f32)
        ident16 = sb("ident16", [128, 128], f16)
        one16 = sb("one16", [128, 1], f16)
        onebf = sb("onebf", [128, 1], bf16)
        minus_half = sb("minus_half", [128, 8], f32)
        peak = sb("peak", [128, 8], f32)
        total = sb("total", [128, 8], f32)
        inverse = sb("inverse", [128, 8], f32)
        q_ms = sb("q_ms", [128, 8], f32)
        q_rms = sb("q_rms", [128, 2, 8], f32)
        k_ms = sb("k_ms", [128, XKV], f32)
        k_rms = sb("k_rms", [128, XKV], f32)
        stats = sb("stats", [128, 2, 6], f32)
        moments = sb("moments", [128, 2, 2], f32)
        ln_var = sb("ln_var", [128, 2], f32)
        ln_rstd = sb("ln_rstd", [128, 2], f32)
        gather = ctx.enter_context(nc.psum_tensor("gather", [128, 512], f32))
        banks = [ctx.enter_context(nc.psum_tensor(f"bank{i}", [128, 512], f32)) for i in range(NBANK)]

        w_qkv = w_a[:, 0:3072].rearrange("p (l k n) -> p l k n", l=2, k=KC)
        w_aout = w_a[:, 3072:4096].rearrange("p (l k n) -> p l k n", l=2, k=KC)
        w_down = w_a[:, :].rearrange("p (e l f n) -> p e l f n", e=2, l=2, f=FC)
        w_up = w_kv[:, :, :, :].rearrange("p e l (k n) -> p e l k n", k=KC)
        w_xq_v = w_xq[:, :, :, :].rearrange("p g l (k n) -> p g l k n", k=KC)
        w_xo_v = w_xo[:, :, :, :].rearrange("p g l (h n) -> p g l h n", h=GH)
        ctx_parts = parts[:, :, :].rearrange("p s (l k n) -> p s l k n", l=2, k=KC)
        hid_parts = parts[:, :, :].rearrange("p l (f n) -> p l f n", f=FC)
        attn_x = attn[:, :, :].rearrange("p l (h n) -> p l h n", h=GH)

        filled = sem("filled")
        freed = {"dve": sem("freed_by_dve"), "act": sem("freed_by_act")}
        s_const = sem("s_const")
        s_rows_in = sem("s_rows_in")
        s_resid = [sem(f"s_resid{t}") for t in range(NT)]
        s_staged = [sem(f"s_staged{i}") for i in range(NSTAGE)]
        s_high = sem("s_high")
        s_low = {False: sem("s_low_dve"), True: sem("s_low_pool")}
        s_zero = sem("s_zero")
        s_made = sem("s_made")
        s_pool_made = sem("s_pool_made")
        s_rows = sem("s_rows")
        s_aq_hi, s_ak_hi, s_av_hi = sem("s_aq_hi"), sem("s_ak_hi"), sem("s_av_hi")
        s_v_hi, s_key_hi, s_attn_hi, s_acts_hi = sem("s_v_hi"), sem("s_key_hi"), sem("s_attn_hi"), sem("s_acts_hi")
        s_q_hi = sem("s_q_hi")
        s_av_copied, s_v_copied = sem("s_av_copied"), sem("s_v_copied")
        s_k_read = sem("s_k_read")
        s_k_sum, s_k_ms, s_k_rms, s_k_normed = sem("s_k_sum"), sem("s_k_ms"), sem("s_k_rms"), sem("s_k_normed")
        s_masked, s_peak, s_shifted, s_exp = sem("s_masked"), sem("s_peak"), sem("s_shifted"), sem("s_exp")
        s_total, s_inverse, s_prob = sem("s_total"), sem("s_inverse"), sem("s_prob")
        s_prob_hi, s_probs = sem("s_prob_hi"), sem("s_probs")
        s_values = sem("s_values")
        s_gather_read = sem("s_gather_read")
        s_sq_hi, s_sq = sem("s_sq_hi"), sem("s_sq")
        s_q_ms, s_q_rms = sem("s_q_ms"), sem("s_q_rms")
        s_stats, s_moments, s_var, s_rstd, s_normed = (
            sem("s_stats"), sem("s_moments"), sem("s_var"), sem("s_rstd"), sem("s_normed"))
        s_logits, s_route0, s_route = sem("s_logits"), sem("s_route0"), sem("s_route")
        s_hid_hi, s_hid = sem("s_hid_hi"), sem("s_hid")
        s_stored = sem("s_stored")

        block = ctx.enter_context(nc.Block())

        def bank_of(job):
            return banks[job % NBANK]

        def job_of(name, k, i=0):
            return FIRST_JOB[name, k] + i

        def wait_filled(eng, job):
            eng.wait_ge(filled, job + 1)

        def wait_bank(eng, job):
            if job >= NBANK:
                engine, count = JOB_ENDS[job - NBANK]
                eng.wait_ge(freed[engine], count)

        def wait_read(eng, job):
            engine, count = JOB_ENDS[job]
            eng.wait_ge(freed[engine], count)

        def wait_item(eng, kind, k=0):
            i = ITEMS.index((kind, k))
            on_pool = LOW_ON_POOL[i]
            eng.wait_ge(s_low[on_pool], sum(LOW_ON_POOL[j] == on_pool for j in range(i + 1)))

        NORMS = [k for name, k in SCHEDULE if name == "norm"]
        TURNS = [k for name, k in SCHEDULE if name == "norm_turn"]
        DOWNS = [k for name, k in SCHEDULE if name == "f_down"]
        UPS = [k for name, k in SCHEDULE if name == "f_up"]

        def norm_no(k):
            return NORMS.index(k)

        def item_parts(i):
            kind, k = ITEMS[i]
            if kind == "x":
                return [acts[:, l, :, k * T:(k + 1) * T] for l in range(2)]
            if kind == "qk":
                return [w_qkv[:, l, :, 0:512] for l in range(2)]
            if kind == "v":
                return [w_qkv[:, l, :, 512:768] for l in range(2)]
            if kind == "ctx":
                return [ctx_parts[:, k % 2, l, :, :] for l in range(2)]
            if kind in ("wk", "wv"):
                return [w_up[:, int(kind == "wv"), l, :, :] for l in range(2)]
            if kind == "aout":
                return [w_aout[:, l, :, :] for l in range(2)]
            if kind == "xq":
                return [w_xq_v[:, k % 2, l, :, :] for l in range(2)]
            if kind == "xo":
                return [w_xo_v[:, k % 2, l, :, :] for l in range(2)]
            if kind == "up":
                return [w_up[:, k, l, :, :] for l in range(2)]
            return [w_down[:, k, l, :, :] for l in range(2)]

        def item_source(i):
            kind, k = ITEMS[i]
            by_chunk = lambda a: a.rearrange("(k p) n -> p k n", p=128)
            if kind == "x":
                return by_chunk(xT)[:, :, k * T:(k + 1) * T]
            if kind == "ctx":
                return by_chunk(ctxT)[:, :, k * T:(k + 1) * T]
            if kind == "qk":
                return by_chunk(wqkvT)[:, :, 0:512]
            if kind == "v":
                return by_chunk(wqkvT)[:, :, 512:768]
            if kind == "xq":
                return by_chunk(Wq)[:, :, k * 512:(k + 1) * 512]
            if kind == "xo":
                return by_chunk(Wo)[:, k * GH:(k + 1) * GH, :]
            return by_chunk({"wk": Wk, "wv": Wv, "aout": woutT, "up": WupT[k], "down": WdownT[k]}[kind])

        def item_stage(i):
            shape = item_source(i).shape
            return stage[:, i % NSTAGE, 0:shape[1] * shape[2]].rearrange("p (k n) -> p k n", k=shape[1])

        def wait_item_room(eng, i):
            kind, k = ITEMS[i]
            if kind == "ctx" and k >= 2:
                wait_filled(eng, job_of("kv_project", 2 * (k - 2) + 1, 1))
            if kind == "xq" and k >= 2:
                wait_filled(eng, job_of("x_query", (k - 2) * NT + NT - 1, 1))
            if kind == "xo" and k >= 2:
                wait_filled(eng, job_of("x_out", (k - 2) * NT + NT - 1))
            if kind == "up":
                wait_filled(eng, job_of("kv_project", NC - 1, 1))
            if kind == "down":
                wait_filled(eng, job_of("a_out", NT - 1))

        def wait_unit_used(eng, n):
            if n >= NA:
                wait_filled(eng, job_of("x_values", n - NA, 1))
            else:
                eng.wait_ge(s_values, n + 1)

        def resid_of(t):
            return resid[:, 2 * t:2 * t + 2, :].rearrange("p j n -> p (j n)")

        def blocks(ap):
            return ap.rearrange("p (k n) -> p k n", n=S)

        def query_slots(ap, h):
            pair = ap[:, h // 2 * 512:(h // 2 + 1) * 512].rearrange("p (b n) -> p b n", b=4)
            return pair[:, :, h % 2 * S:(h % 2 + 1) * S]

        def each_block(ap):
            return ap.unsqueeze(2).to_broadcast([128, 8, S])

        def all_blocks(ap):
            return ap.unsqueeze(1).to_broadcast([128, 8, S])

        def prob_part(n, low, parity):
            at = S if low != bool(parity) else 0
            return probs[:, n % 2, 4 * parity:4 * parity + 4, at:at + S]

        @block.sync
        def _(sp):
            for i in range(len(ITEMS)):
                if i == 4:
                    for t in range(NT):
                        sp.dma_start(resid[:, 2 * t:2 * t + 2, :],
                                     x[t * T:(t + 1) * T, :].rearrange("(j p) n -> p j n", p=128))\
                            .then_inc(s_resid[t], 16)
                if i >= NSTAGE:
                    on_pool = LOW_ON_POOL[i - NSTAGE]
                    sp.wait_ge(s_low[on_pool], sum(LOW_ON_POOL[j] == on_pool for j in range(i - NSTAGE + 1)))
                sp.dma_start(item_stage(i), item_source(i)).then_inc(s_staged[i % NSTAGE], 16)
            for name, k in SCHEDULE:
                if name == "store":
                    sp.wait_ge(s_normed, norm_no((2, k)) + 1)
                    sp.dma_start(out[k * T:(k + 1) * T, :].rearrange("(j p) n -> p j n", p=128),
                                 resid[:, 2 * k:2 * k + 2, :]).then_inc(s_stored, 16)
            sp.wait_ge(s_stored, 16 * NT)

        @block.scalar
        def _(act):
            for dst, src in ((cols[:, :], columns), (ident[:, :], identity), (causal_sb[0:64, :], causal),
                             (causal_sb[64:128, :], causal), (mask_sb[0:64, :], mask),
                             (mask_sb[64:128, :], mask),
                             (gate_sb[:, :, :], gate_w.partition_broadcast(128))):
                act.dma_start(dst, src).then_inc(s_const, 16)
            act.wait_ge(s_zero, 1)
            for part in range(2):
                act.dma_start(scores[part:part + 97:32, 0:2, :].rearrange("p a n -> p (a n)")[:, 0:RW],
                              bias_rows).then_inc(s_rows_in, 16)
            act.wait_ge(s_const, 16 * 7)

            for name, k in SCHEDULE:
                if name == "load":
                    act.wait_ge(s_staged[k % NSTAGE], 16 * (k // NSTAGE + 1))
                    wait_item_room(act, k)
                    act.activation(item_parts(k)[0], item_stage(k), ACT.Copy).then_inc(s_high, 1)

                elif name == "a_project":
                    job = job_of(name, k)
                    wait_filled(act, job)
                    if k:
                        wait_filled(act, job_of("a_scores", 4 * k - 1))
                    for e in range(2):
                        act.activation(a_q[:, 0, :, e * S:(e + 1) * S], blocks(bank_of(job)[:, :]), ACT.Copy,
                                       scale=cols[:, C_HEAD + e:C_HEAD + e + 1]).then_inc(s_aq_hi, 1)
                    wait_filled(act, job + 1)
                    act.activation(a_k[:, 0, :], bank_of(job + 1)[:, :], ACT.Copy).then_inc(s_ak_hi, 1)
                    wait_filled(act, job + 2)
                    act.wait_ge(s_zero, 2)
                    if k:
                        act.wait_ge(s_av_copied, 16 * 8 * k)
                    bank = bank_of(job + 2)[:, :].rearrange("p (j i n) -> p j i n", j=2, n=2 * SD)
                    for e in range(2):
                        spread = v_spread[:, :, 0, :].rearrange("p j (i n) -> p j i n", n=4 * SD)
                        act.activation(spread[:, :, :, 3 * SD * e:3 * SD * e + SD],
                                       bank[:, :, :, SD * e:SD * e + SD], ACT.Copy).then_inc(s_av_hi, 1)

                elif name == "v_copies":
                    wait_read(act, job_of("a_project", k, 2))
                    act.wait_ge(s_made, 5)
                    if k:
                        wait_unit_used(act, 4 * k - 1)
                    for j in range(2):
                        for b, lo, hi in ((2 * j, 0, 64), (2 * j + 1, 64, 128)):
                            other = slice(64 - lo, 128 - lo)
                            act.dma_start(a_values_sb[lo:hi, b, :, :], v_spread[lo:hi, j, :, :])\
                                .then_inc(s_av_copied, 16)
                            act.dma_start(a_values_sb[other, b, 0, :], v_spread[lo:hi, j, 0, :])\
                                .then_inc(s_av_copied, 16)

                elif name == "kv_project":
                    job = job_of(name, k)
                    wait_filled(act, job)
                    if k:
                        act.wait_ge(s_k_sum, k)
                    act.activation(k_sq[:, :], bank_of(job)[:, :], ACT.Square).then_inc(s_k_read, 1)
                    wait_filled(act, job + 1)
                    if k:
                        act.wait_ge(s_v_copied, 16 * 4 * k)
                    act.activation(v_parts[:, 0, :], bank_of(job + 1)[:, :], ACT.Copy).then_inc(s_v_hi, 1)

                elif name == "k_turn":
                    wait_read(act, job_of("kv_project", k, 1))
                    act.wait_ge(s_zero, 3)
                    for b, lo, hi in ((2 * k, 0, 64), (2 * k + 1, 64, 128)):
                        other = slice(64 - lo, 128 - lo)
                        act.dma_start(values[lo:hi, b, :, :], v_parts[lo:hi, :, :]).then_inc(s_v_copied, 16)
                        act.dma_start(values[other, b, 0, :], v_parts[lo:hi, 0, :]).then_inc(s_v_copied, 16)
                    job = job_of(name, k)
                    wait_filled(act, job)
                    act.wait_ge(s_made, 8)
                    act.activation(keys[:, 0, :, k * 128:(k + 1) * 128],
                                   bank_of(job)[:, :].rearrange("p (g n) -> p g n", g=XKV), ACT.Copy,
                                   scale=key_scale[:, 0:1]).then_inc(s_key_hi, 1)

                elif name == "soft_m":
                    act.wait_ge(s_shifted, k + 1)
                    act.activation(scores[:, k % 2, :], scores[:, k % 2, :], ACT.Exp).then_inc(s_exp, 1)

                elif name == "soft_c":
                    act.wait_ge(s_prob, k + 1)
                    if k >= 2:
                        wait_filled(act, job_of("turn", k - 2))
                    for parity in range(2):
                        act.activation(prob_part(k, False, parity),
                                       blocks(scores[:, k % 2, :])[:, 4 * parity:4 * parity + 4, :],
                                       ACT.Copy).then_inc(s_prob_hi, 1)

                elif name == "turn":
                    job = job_of(name, k)
                    wait_filled(act, job)
                    if k >= 2:
                        wait_unit_used(act, k - 2)
                    turned = act.activation(probsT[:, k % 2, :, :].rearrange("p k n -> p (k n)"),
                                            bank_of(job)[:, :].bitcast(f16), ACT.Copy)
                    turned.then_inc(freed["act"], 1)

                elif name == "a_split":
                    wait_unit_used(act, 4 * k + 3)
                    if k:
                        wait_filled(act, job_of("a_out", k - 1))
                    act.activation(attn[:, 0, 0:512], gather[:, :], ACT.Copy)\
                        .then_inc(s_attn_hi, 1)

                elif name == "norm_turn":
                    job = job_of(name, k)
                    wait_filled(act, job)
                    act.activation(acts[:, 0, :, k[1] * T:(k[1] + 1) * T],
                                   bank_of(job)[:, :].rearrange("p (k n) -> p k n", k=KC), ACT.Copy)\
                        .then_inc(s_acts_hi, 1)

                elif name == "x_query":
                    g = k // NT
                    if k == 0:
                        wait_unit_used(act, NA - 1)
                    if k >= 2:
                        wait_filled(act, job_of("x_scores", k - 2))
                    for pair in range(2):
                        job = job_of(name, k, pair)
                        wait_filled(act, job)
                        if k and pair == 0:
                            act.wait_ge(s_sq, k)
                        for e in range(2):
                            h = 2 * pair + e
                            bias = cols[:, C_BQ + GH * g + h:C_BQ + GH * g + h + 1]
                            head = blocks(bank_of(job)[:, e * T:(e + 1) * T])
                            act.activation(query_slots(queries[:, k % 2, 0, :], h), head, ACT.Identity,
                                           bias=bias).then_inc(s_q_hi, 1)
                            act.activation(query_slots(sq, h), head, ACT.Square, bias=bias)\
                                .then_inc(s_q_hi, 1)

                elif name == "x_values":
                    for parity in range(2):
                        job = job_of(name, k, parity)
                        wait_filled(act, job)
                        if parity == 0:
                            wait_filled(act, job_of("x_out", k - 1) if k else job_of("a_out", NT - 1))
                        act.activation(
                            attn_x[:, 0, :, :].rearrange("p h (c r q) -> p r c h q", r=2, q=S)[:, parity],
                            bank_of(job)[:, :].rearrange("p (c h q) -> p c h q", h=GH, q=S), ACT.Copy)\
                            .then_inc(s_attn_hi, 1)

                elif name == "f_up":
                    t, e, f = k
                    job, n = job_of(name, k), UPS.index(k)
                    wait_filled(act, job)
                    if n >= 2:
                        act.wait_ge(s_hid, n - 1)
                    else:
                        wait_filled(act, job_of("k_turn", NC - 1))
                    for i in range(2):
                        c = C_BUP + FC * e + 2 * f + i
                        done = act.activation(hidden[n % 2][:, i * T:(i + 1) * T],
                                              bank_of(job)[:, i * T:(i + 1) * T],
                                              ACT.Relu if e else ACT.Gelu, bias=cols[:, c:c + 1])
                    done.then_inc(freed["act"], 1)

        @block.vector
        def _(dve):
            dve.memset(scores[:, :, :], 0.0).then_inc(s_zero, 1)
            dve.memset(v_spread[:, :, :, :], 0.0).then_inc(s_zero, 1)
            dve.memset(values[:, :, 1, :], 0.0).then_inc(s_zero, 1)
            dve.memset(ones[:, :].bitcast(f32), 1.0).then_inc(s_made, 1)
            dve.memset(minus_half[:, :], -0.5).then_inc(s_made, 1)
            dve.memset(one16[:, :], 1.0).then_inc(s_made, 1)
            dve.memset(onebf[:, :], 1.0).then_inc(s_made, 1)
            dve.memset(a_values_sb[:, :, 1, :], 0.0).then_inc(s_made, 1)
            dve.wait_ge(s_const, 16 * 7)
            dve.tensor_copy(ident16[:, :], ident[:, :]).then_inc(s_made, 1)
            dve.tensor_tensor(key_scale[:, :], cols[:, C_QN:C_QN + 1], cols[:, C_KN:C_KN + 1], ALU.mult)\
                .then_inc(s_made, 1)
            dve.wait_ge(s_made, 7)
            dve.tensor_scalar(key_scale[:, :], key_scale[:, :], float(XD) ** -0.5, None, ALU.mult)\
                .then_inc(s_made, 1)
            dve.wait_ge(s_rows_in, 32)
            raw = scores[:, :, :].rearrange("p a n -> p (a n)")[:, 0:RW]
            rounded = w_xq[:, 1, 1, 0:RW]
            dve.tensor_copy(rounded, raw).then_inc(s_rows, 1)
            dve.wait_ge(s_rows, 1)
            dve.scalar_tensor_tensor(rows[:, :], rounded.bitcast(f32), cols[:, C_SECOND:C_SECOND + 1], raw,
                                     ALU.mult, ALU.add).then_inc(s_rows, 1)

            for name, k in SCHEDULE:
                if name == "load":
                    if not LOW_ON_POOL[k]:
                        dve.wait_ge(s_high, k + 1)
                        dve.tensor_tensor(item_parts(k)[1], item_stage(k), item_parts(k)[0].bitcast(f32),
                                          ALU.subtract).then_inc(s_low[False], 1)

                elif name == "a_project":
                    job = job_of(name, k)
                    dve.wait_ge(s_aq_hi, 2 * (k + 1))
                    for e in range(2):
                        done = dve.scalar_tensor_tensor(
                            a_q[:, 1, :, e * S:(e + 1) * S], blocks(bank_of(job)[:, :]),
                            cols[:, C_HEAD + e:C_HEAD + e + 1], a_q[:, 0, :, e * S:(e + 1) * S],
                            ALU.mult, ALU.subtract)
                    done.then_inc(freed["dve"], 1)
                    dve.wait_ge(s_ak_hi, k + 1)
                    dve.tensor_tensor(a_k[:, 1, :], bank_of(job + 1)[:, :], a_k[:, 0, :], ALU.subtract)\
                        .then_inc(freed["dve"], 1)
                    dve.wait_ge(s_av_hi, 2 * (k + 1))
                    bank = bank_of(job + 2)[:, :].rearrange("p (j i n) -> p j i n", j=2, n=2 * SD)
                    spread = v_spread[:, :, :, :].rearrange("p j l (i n) -> p l j i n", n=4 * SD)
                    for e in range(2):
                        to = slice(3 * SD * e, 3 * SD * e + SD)
                        done = dve.tensor_tensor(spread[:, 1, :, :, to], bank[:, :, :, SD * e:SD * e + SD],
                                                 spread[:, 0, :, :, to], ALU.subtract)
                    done.then_inc(freed["dve"], 1)

                elif name == "kv_project":
                    job = job_of(name, k)
                    dve.wait_ge(s_k_read, k + 1)
                    if k:
                        wait_filled(dve, job_of("k_turn", k - 1))
                    dve.tensor_copy(k_raw[:, :], bank_of(job)[:, :]).then_inc(freed["dve"], 1)
                    if k:
                        dve.wait_ge(s_k_rms, k)
                    dve.tensor_reduce(k_ms[:, :], k_sq[:, :].rearrange("p (g n) -> p g n", g=XKV), AX.X,
                                      ALU.add).then_inc(s_k_sum, 1)
                    dve.wait_ge(s_k_sum, k + 1)
                    dve.tensor_scalar(k_ms[:, :], k_ms[:, :], 1.0 / XD, RMS_EPS, ALU.mult, ALU.add)\
                        .then_inc(s_k_ms, 1)
                    dve.wait_ge(s_v_hi, k + 1)
                    dve.tensor_tensor(v_parts[:, 1, :], bank_of(job + 1)[:, :], v_parts[:, 0, :],
                                      ALU.subtract).then_inc(freed["dve"], 1)

                elif name == "k_turn":
                    dve.wait_ge(s_key_hi, k + 1)
                    at = slice(k * 128, (k + 1) * 128)
                    dve.scalar_tensor_tensor(
                        keys[:, 1, :, at], bank_of(job_of(name, k))[:, :].rearrange("p (g n) -> p g n", g=XKV),
                        key_scale[:, 0:1], keys[:, 0, :, at], ALU.mult, ALU.subtract).then_inc(freed["dve"], 1)

                elif name == "soft_a":
                    if k >= 2:
                        dve.wait_ge(s_probs, k - 1)
                    if k < NA:
                        job = job_of("a_scores", k)
                        wait_filled(dve, job)
                        dve.scalar_tensor_tensor(blocks(scores[:, k % 2, :]), blocks(bank_of(job)[:, :]),
                                                 float(SD) ** -0.5, all_blocks(causal_sb[:, :]),
                                                 ALU.mult, ALU.add).then_inc(freed["dve"], 1)
                    else:
                        u = k - NA
                        job = job_of("x_scores", u)
                        wait_filled(dve, job)
                        dve.wait_ge(s_q_rms, u + 1)
                        dve.tensor_tensor(blocks(scores[:, k % 2, :]), blocks(bank_of(job)[:, :]),
                                          each_block(q_rms[:, u % 2, :]), ALU.mult).then_inc(freed["dve"], 1)

                elif name == "soft_m":
                    if k < NA:
                        wait_read(dve, job_of("a_scores", k))
                    else:
                        dve.wait_ge(s_masked, k - NA + 1)
                    if k:
                        dve.wait_ge(s_shifted, k)
                    dve.tensor_reduce(peak[:, :], blocks(scores[:, k % 2, :]), AX.X, ALU.max)\
                        .then_inc(s_peak, 1)

                elif name == "soft_b":
                    dve.wait_ge(s_exp, k + 1)
                    dve.tensor_reduce(total[:, :], blocks(scores[:, k % 2, :]), AX.X, ALU.add)\
                        .then_inc(s_total, 1)
                    dve.wait_ge(s_total, k + 1)
                    if k:
                        dve.wait_ge(s_prob, k)
                    dve.reciprocal(inverse[:, :], total[:, :]).then_inc(s_inverse, 1)

                elif name == "soft_c":
                    dve.wait_ge(s_prob_hi, 2 * (k + 1))
                    for parity in range(2):
                        done = dve.tensor_tensor(
                            prob_part(k, True, parity),
                            blocks(scores[:, k % 2, :])[:, 4 * parity:4 * parity + 4, :],
                            prob_part(k, False, parity), ALU.subtract)
                    done.then_inc(s_probs, 1)

                elif name == "a_split":
                    dve.wait_ge(s_attn_hi, k + 1)
                    dve.tensor_tensor(attn[:, 1, 0:512], gather[:, :], attn[:, 0, 0:512].bitcast(f32),
                                      ALU.subtract).then_inc(s_gather_read, 1)

                elif name == "a_out":
                    job = job_of(name, k)
                    wait_filled(dve, job)
                    dve.wait_ge(s_resid[k], 16)
                    dve.tensor_tensor(resid_of(k), bank_of(job)[:, :], resid_of(k), ALU.add)\
                        .then_inc(freed["dve"], 1)

                elif name == "norm":
                    w, t = k
                    wait_read(dve, (job_of("a_out", t), job_of("x_out", NX - NT + t) if w else 0,
                                    job_of("f_down", (t, 1)) if w else 0)[w])
                    n = norm_no(k)
                    if n:
                        dve.wait_ge(s_normed, n)
                    for j in range(2):
                        dve.bn_stats(stats[:, j, :], resid[:, 2 * t + j, :]).then_inc(s_stats, 1)
                    dve.wait_ge(s_stats, 2 * n + 2)
                    for j in range(2):
                        dve.bn_aggr(moments[:, j, :], stats[:, j, :]).then_inc(s_moments, 1)
                    dve.wait_ge(s_moments, 2 * n + 2)
                    dve.tensor_scalar(ln_var[:, :], moments[:, :, 1], LN_EPS, None, ALU.add).then_inc(s_var, 1)

                elif name == "norm_end":
                    t = k[1]
                    dve.wait_ge(s_rstd, norm_no(k) + 1)
                    for j in range(2):
                        done = dve.tensor_scalar(resid[:, 2 * t + j, :], resid[:, 2 * t + j, :],
                                                 moments[:, j, 0:1], ln_rstd[:, j:j + 1],
                                                 ALU.subtract, ALU.mult)
                    done.then_inc(s_normed, 1)

                elif name == "norm_turn":
                    wait_high = TURNS.index(k) + 1
                    dve.wait_ge(s_acts_hi, wait_high)
                    at = slice(k[1] * T, (k[1] + 1) * T)
                    dve.tensor_tensor(acts[:, 1, :, at],
                                      bank_of(job_of(name, k))[:, :].rearrange("p (k n) -> p k n", k=KC),
                                      acts[:, 0, :, at].bitcast(f32), ALU.subtract).then_inc(freed["dve"], 1)

                elif name == "x_query":
                    g = k // NT
                    for pair in range(2):
                        job = job_of(name, k, pair)
                        dve.wait_ge(s_q_hi, 8 * k + 4 * pair + 4)
                        for e in range(2):
                            h = 2 * pair + e
                            done = dve.scalar_tensor_tensor(
                                query_slots(queries[:, k % 2, 1, :], h), blocks(bank_of(job)[:, e * T:(e + 1) * T]),
                                cols[:, C_BQ + GH * g + h:C_BQ + GH * g + h + 1],
                                query_slots(queries[:, k % 2, 0, :], h), ALU.add, ALU.subtract)
                        done.then_inc(freed["dve"], 1)

                elif name == "x_squares":
                    job = job_of(name, k)
                    wait_filled(dve, job)
                    if k:
                        dve.wait_ge(s_q_rms, k)
                    dve.tensor_scalar(q_ms[:, :], bank_of(job)[:, 0:8], 1.0 / XD, RMS_EPS, ALU.mult, ALU.add)\
                        .then_inc(freed["dve"], 1)

                elif name == "x_values":
                    for parity in range(2):
                        dve.wait_ge(s_attn_hi, NT + 2 * k + parity + 1)
                        at = lambda l: attn_x[:, l, :, :].rearrange(
                            "p h (c r q) -> p r c h q", r=2, q=S)[:, parity]
                        dve.tensor_tensor(
                            at(1), bank_of(job_of(name, k, parity))[:, :].rearrange("p (c h q) -> p c h q", h=GH, q=S),
                            at(0).bitcast(f32), ALU.subtract).then_inc(freed["dve"], 1)

                elif name == "x_out":
                    t = k % NT
                    job = job_of(name, k)
                    wait_filled(dve, job)
                    if k < NT:
                        dve.wait_ge(s_normed, norm_no((0, t)) + 1)
                    else:
                        wait_read(dve, job_of(name, k - NT))
                    dve.tensor_tensor(resid_of(t), bank_of(job)[:, :], resid_of(t), ALU.add)\
                        .then_inc(freed["dve"], 1)

                elif name == "gate":
                    dve.wait_ge(s_normed, norm_no((1, k)) + 1)
                    for j in range(2):
                        for e in range(2):
                            dve.tensor_tensor_reduce(gate_junk[:, :], resid[:, 2 * k + j, :], gate_sb[:, e, :],
                                                     1.0, 0.0, ALU.mult, ALU.add, logits[:, j, e:e + 1])\
                                .then_inc(s_logits, 1)
                            dve.wait_ge(s_logits, 4 * k + 2 * j + e + 1)
                    dve.tensor_tensor(routed[:, :, 0], logits[:, :, 0], logits[:, :, 1], ALU.is_ge)\
                        .then_inc(s_route0, 1)
                    dve.wait_ge(s_route0, k + 1)
                    dve.tensor_scalar(routed[:, :, 1], routed[:, :, 0], -1.0, 1.0, ALU.mult, ALU.add)\
                        .then_inc(s_route, 1)

                elif name == "f_up":
                    t, e, f = k
                    n = UPS.index(k)
                    dve.wait_ge(s_hid_hi, n + 1)
                    at = slice(f * 512, (f + 1) * 512)
                    dve.tensor_tensor(parts[:, 1, at], hidden[n % 2][:, :], parts[:, 0, at].bitcast(f32),
                                      ALU.subtract).then_inc(s_hid, 1)

                elif name == "f_down":
                    t, e = k
                    job = job_of(name, k)
                    wait_filled(dve, job)
                    dve.wait_ge(s_route, t + 1)
                    if e:
                        wait_read(dve, job_of(name, (t, 0)))
                    for j in range(2):
                        done = dve.scalar_tensor_tensor(resid[:, 2 * t + j, :], bank_of(job)[:, j * D:(j + 1) * D],
                                                        routed[:, j, e:e + 1], resid[:, 2 * t + j, :],
                                                        ALU.mult, ALU.add)
                    done.then_inc(freed["dve"], 1)

        @block.gpsimd
        def _(pool):
            for name, k in SCHEDULE:
                if name == "load":
                    if LOW_ON_POOL[k]:
                        pool.wait_ge(s_high, k + 1)
                        pool.tensor_tensor(item_parts(k)[1], item_stage(k), item_parts(k)[0].bitcast(f32),
                                           ALU.subtract).then_inc(s_low[True], 1)

                elif name == "kv_project":
                    pool.wait_ge(s_k_ms, k + 1)
                    pool.wait_ge(s_made, 2)
                    pool.tensor_tensor(k_rms[:, :], k_ms[:, :], minus_half[:, 0:XKV], ALU.pow)\
                        .then_inc(s_k_rms, 1)
                    pool.wait_ge(s_k_rms, k + 1)
                    by_head = k_raw[:, :].rearrange("p (g n) -> p g n", g=XKV)
                    pool.tensor_tensor(by_head, by_head, k_rms[:, :].unsqueeze(2).to_broadcast([128, XKV, XD]),
                                       ALU.mult).then_inc(s_k_normed, 1)

                elif name == "soft_a" and k >= NA:
                    wait_read(pool, job_of("x_scores", k - NA))
                    at = blocks(scores[:, k % 2, :])
                    pool.tensor_tensor(at, at, all_blocks(mask_sb[:, :]), ALU.add).then_inc(s_masked, 1)

                elif name == "soft_m":
                    pool.wait_ge(s_peak, k + 1)
                    at = blocks(scores[:, k % 2, :])
                    pool.tensor_tensor(at, at, each_block(peak[:, :]), ALU.subtract).then_inc(s_shifted, 1)

                elif name == "soft_b":
                    pool.wait_ge(s_inverse, k + 1)
                    at = blocks(scores[:, k % 2, :])
                    pool.tensor_tensor(at, at, each_block(inverse[:, :]), ALU.mult).then_inc(s_prob, 1)

                elif name == "norm":
                    pool.wait_ge(s_var, norm_no(k) + 1)
                    pool.tensor_tensor(ln_rstd[:, :], ln_var[:, :], minus_half[:, 0:2], ALU.pow)\
                        .then_inc(s_rstd, 1)

                elif name == "x_query":
                    pool.wait_ge(s_q_hi, 8 * (k + 1))
                    if k:
                        wait_filled(pool, job_of("x_squares", k - 1))
                    pool.tensor_scalar(sq_hi, sq, 1.0, 0.0, ALU.mult, ALU.add).then_inc(s_sq_hi, 1)
                    pool.wait_ge(s_sq_hi, k + 1)
                    pool.tensor_tensor(sq_lo, sq, sq_hi, ALU.subtract).then_inc(s_sq, 1)

                elif name == "x_squares":
                    wait_read(pool, job_of(name, k))
                    if k >= 2:
                        wait_read(pool, job_of("x_scores", k - 2))
                    pool.tensor_tensor(q_rms[:, k % 2, :], q_ms[:, :], minus_half[:, :], ALU.pow)\
                        .then_inc(s_q_rms, 1)

                elif name == "f_up":
                    t, e, f = k
                    n = UPS.index(k)
                    wait_read(pool, job_of(name, k))
                    before = DOWNS.index((t, e)) - 1
                    if before >= 0:
                        wait_filled(pool, job_of("f_down", DOWNS[before]))
                    else:
                        wait_filled(pool, job_of("kv_project", NC - 1, 1))
                    pool.tensor_scalar(parts[:, 0, f * 512:(f + 1) * 512], hidden[n % 2][:, :], 1.0, 0.0,
                                       ALU.mult, ALU.add).then_inc(s_hid_hi, 1)

        @block.tensor
        def _(pe):
            def bias(out_ap, row, width, tokens_first, col=0):
                group, first = row
                at = slice(32 * group, 32 * group + 2)
                bias_row = rows[at, first + col:first + col + width]
                if tokens_first:
                    pe.matmul(out_ap, ones[at, 0:128], bias_row, start=True, stop=False)
                else:
                    pe.matmul(out_ap, bias_row, ones[at, 0:T], start=True, stop=False)

            def product(out_ap, still, moving, chunks, start):
                for c in range(chunks):
                    for i, (a, b) in enumerate(SPLITS):
                        done = pe.matmul(out_ap, still(a, c), moving(b, c), start=start and c == 0 and i == 0,
                                         stop=c == chunks - 1 and i == len(SPLITS) - 1)
                return done

            pe.wait_ge(s_made, 8)
            pe.wait_ge(s_rows, 2)
            for name, k in SCHEDULE:
                if name == "a_project":
                    wait_item(pe, "x", k)
                    wait_item(pe, "qk")
                    tile = slice(k * T, (k + 1) * T)
                    for which in range(2):
                        job = job_of(name, k, which)
                        wait_bank(pe, job)
                        for c in range(2):
                            to, col = bank_of(job)[:, c * T:(c + 1) * T], which * D + c * 128
                            bias(to, R_QKV, 128, False, col)
                            done = product(to, lambda l, q: w_qkv[:, l, q, col:col + 128],
                                           lambda l, q: acts[:, l, q, tile], KC, False)
                        done.then_inc(filled, 1)
                    wait_item(pe, "v")
                    job = job_of(name, k, 2)
                    wait_bank(pe, job)
                    for j in range(2):
                        to, tok = bank_of(job)[:, j * D:(j + 1) * D], k * T + j * 128
                        bias(to, R_QKV, D, True, 2 * D)
                        done = product(to, lambda l, q: acts[:, l, q, tok:tok + 128],
                                       lambda l, q: w_qkv[:, l, q, 2 * D:3 * D], KC, False)
                    done.then_inc(filled, 1)

                elif name == "a_scores":
                    job = job_of(name, k)
                    wait_read(pe, job_of("a_project", k // 4, 1))
                    wait_bank(pe, job)
                    rows32 = slice(32 * (k % 4), 32 * (k % 4) + 32)
                    for b in range(4):
                        for i in range(2):
                            tok = slice(i * T + b * S, i * T + (b + 1) * S)
                            at = block_of(b, i)
                            done = product(bank_of(job)[:, at * S:(at + 1) * S],
                                           lambda l, _: a_q[rows32, l, 4 * i + b, :],
                                           lambda l, _: a_k[rows32, l, tok], 1, True)
                    done.then_inc(filled, 1)

                elif name == "turn":
                    job = job_of(name, k)
                    pe.wait_ge(s_probs, k + 1)
                    wait_bank(pe, job)
                    turned = bank_of(job)[:, :].bitcast(f16)
                    for at in range(8):
                        done = pe.transpose(turned[:, at * 128:(at + 1) * 128], probs[:, k % 2, at, :],
                                            ident16[:, :])
                    done.then_inc(filled, 1)

                elif name == "a_values":
                    t, r = k // 4, k % 4
                    wait_read(pe, job_of("turn", k))
                    if r == 0:
                        pe.wait_ge(s_av_copied, 16 * 8 * (t + 1))
                        if t:
                            pe.wait_ge(s_gather_read, t)
                    for b in range(4):
                        for i in range(2):
                            to = gather[32 * r:32 * r + 32, i * T + b * S:i * T + (b + 1) * S]
                            for e in range(2):
                                at = (4 * i + r) * 4 * SD + e * 2 * SD
                                for l in range(2):
                                    done = pe.matmul(to, a_values_sb[:, b, l, at:at + 2 * SD],
                                                     probsT[:, k % 2, block_of(b, i), e * S:(e + 1) * S],
                                                     start=e == 0 and l == 0, stop=e == 1 and l == 1)
                    done.then_inc(s_values, 1)

                elif name == "a_out":
                    job = job_of(name, k)
                    wait_item(pe, "aout")
                    pe.wait_ge(s_gather_read, k + 1)
                    wait_bank(pe, job)
                    for j in range(2):
                        to = bank_of(job)[:, j * D:(j + 1) * D]
                        bias(to, R_OUT, D, True)
                        done = product(to, lambda l, c: attn[:, l, c * T + j * 128:c * T + (j + 1) * 128],
                                       lambda l, c: w_aout[:, l, c, :], KC, False)
                    done.then_inc(filled, 1)

                elif name == "norm_turn":
                    job = job_of(name, k)
                    pe.wait_ge(s_normed, norm_no(k) + 1)
                    wait_bank(pe, job)
                    for c in range(KC):
                        for j in range(2):
                            done = pe.transpose(bank_of(job)[:, c * T + j * 128:c * T + (j + 1) * 128],
                                                resid[:, 2 * k[1] + j, c * 128:(c + 1) * 128], ident[:, :])
                    done.then_inc(filled, 1)

                elif name == "kv_project":
                    slot, at = (k // 2) % 2, slice((k % 2) * 128, (k % 2) * 128 + 128)
                    wait_item(pe, "ctx", k // 2)
                    for which in range(2):
                        job = job_of(name, k, which)
                        wait_item(pe, ("wk", "wv")[which])
                        wait_bank(pe, job)
                        bias(bank_of(job)[:, :], (R_K, R_V)[which], 512, True)
                        product(bank_of(job)[:, :], lambda l, c: ctx_parts[:, slot, l, c, at],
                                lambda l, c: w_up[:, which, l, c, :], KC, False).then_inc(filled, 1)

                elif name == "k_turn":
                    job = job_of(name, k)
                    pe.wait_ge(s_k_normed, k + 1)
                    wait_bank(pe, job)
                    for g in range(XKV):
                        done = pe.transpose(bank_of(job)[:, g * 128:(g + 1) * 128],
                                            k_raw[:, g * 128:(g + 1) * 128], ident[:, :])
                    done.then_inc(filled, 1)

                elif name == "x_query":
                    g, t = k // NT, k % NT
                    wait_item(pe, "xq", g)
                    wait_read(pe, job_of("norm_turn", (0, t)))
                    for pair in range(2):
                        job = job_of(name, k, pair)
                        wait_bank(pe, job)
                        for e in range(2):
                            h = 2 * pair + e
                            done = product(bank_of(job)[:, e * T:(e + 1) * T],
                                           lambda l, c: w_xq_v[:, g % 2, l, c, h * 128:(h + 1) * 128],
                                           lambda l, c: acts[:, l, c, t * T:(t + 1) * T], KC, True)
                        done.then_inc(filled, 1)

                elif name == "x_squares":
                    job = job_of(name, k)
                    pe.wait_ge(s_sq, k + 1)
                    wait_bank(pe, job)
                    for b in range(4):
                        for i in range(2):
                            at = block_of(b, i)
                            slot = slice((4 * i + b) * 128, (4 * i + b + 1) * 128)
                            pe.matmul(bank_of(job)[:, at:at + 1], sq_hi[:, slot], onebf[:, :],
                                      start=True, stop=False)
                            done = pe.matmul(bank_of(job)[:, at:at + 1], sq_lo[:, slot], one16[:, :],
                                             start=False, stop=True)
                    done.then_inc(filled, 1)

                elif name == "x_scores":
                    g, t = k // NT, k % NT
                    job = job_of(name, k)
                    wait_read(pe, job_of("x_query", k, 1))
                    wait_read(pe, job_of("k_turn", 2 * t + 1))
                    wait_bank(pe, job)
                    for b in range(4):
                        for i in range(2):
                            at, tok = block_of(b, i), (4 * t + b) * S
                            slot = slice((4 * i + b) * 128, (4 * i + b + 1) * 128)
                            done = product(bank_of(job)[:, at * S:(at + 1) * S],
                                           lambda l, _: queries[:, k % 2, l, slot],
                                           lambda l, _: keys[:, l, g, tok:tok + S], 1, True)
                    done.then_inc(filled, 1)

                elif name == "x_values":
                    g, t = k // NT, k % NT
                    wait_read(pe, job_of("turn", NA + k))
                    pe.wait_ge(s_v_copied, 16 * 4 * NC)
                    for parity in range(2):
                        job = job_of(name, k, parity)
                        wait_bank(pe, job)
                        for c in range(2):
                            b = 2 * c + parity
                            at = block_of(b, 0)
                            for l in range(2):
                                done = pe.matmul(bank_of(job)[:, c * T:(c + 1) * T],
                                                 values[:, 4 * t + b, l, g * XD:(g + 1) * XD],
                                                 probsT[:, k % 2, at:at + 2, :], start=l == 0, stop=l == 1)
                        done.then_inc(filled, 1)

                elif name == "x_out":
                    g, t = k // NT, k % NT
                    job = job_of(name, k)
                    wait_item(pe, "xo", g)
                    wait_read(pe, job_of("x_values", k, 1))
                    wait_bank(pe, job)
                    for j in range(2):
                        done = product(bank_of(job)[:, j * D:(j + 1) * D],
                                       lambda l, h: attn_x[:, l, h, j * 128:(j + 1) * 128],
                                       lambda l, h: w_xo_v[:, g % 2, l, h, :], GH, True)
                    done.then_inc(filled, 1)

                elif name == "f_up":
                    t, e, f = k
                    job = job_of(name, k)
                    wait_item(pe, "up", e)
                    wait_read(pe, job_of("norm_turn", (1, t)))
                    wait_bank(pe, job)
                    for i in range(2):
                        col = (2 * f + i) * 128
                        done = product(bank_of(job)[:, i * T:(i + 1) * T],
                                       lambda l, c: w_up[:, e, l, c, col:col + 128],
                                       lambda l, c: acts[:, l, c, t * T:(t + 1) * T], KC, True)
                    done.then_inc(filled, 1)

                elif name == "f_down":
                    t, e = k
                    job = job_of(name, k)
                    wait_item(pe, "down", e)
                    pe.wait_ge(s_hid, UPS.index((t, e, 1)) + 1)
                    wait_bank(pe, job)
                    for j in range(2):
                        to = bank_of(job)[:, j * D:(j + 1) * D]
                        bias(to, R_DOWN[e], D, True)
                        done = product(to, lambda l, c: hid_parts[:, l, c, j * 128:(j + 1) * 128],
                                       lambda l, c: w_down[:, e, l, c, :], FC, False)
                    done.then_inc(filled, 1)


def kernel(x, ctx_2048, mask_1xSxS2_ff0, L0_attn_w_qkv, L0_attn_b_qkv, L0_attn_w_out, L0_attn_b_out,
           L0_xattn_Wq, L0_xattn_bq, L0_xattn_Wk, L0_xattn_bk, L0_xattn_Wv, L0_xattn_bv, L0_xattn_Wo,
           L0_xattn_qn_w, L0_xattn_kn_w, L0_ffn_Wg, L0_ffn_W0a, L0_ffn_b0a, L0_ffn_W0b, L0_ffn_b0b,
           L0_ffn_W1a, L0_ffn_b1a, L0_ffn_W1b, L0_ffn_b1b):
    import numpy as np
    import concourse.bacc as bacc
    from concourse.bass_utils import run_bass_kernel_spmd

    host = np.asarray
    b_qkv, b_out, bk, bv = host(L0_attn_b_qkv), host(L0_attn_b_out), host(L0_xattn_bk), host(L0_xattn_bv)
    b0b, b1b = host(L0_ffn_b0b), host(L0_ffn_b1b)
    f4 = np.float32
    row = np.arange(128)
    head = np.stack([(row // SD) % 2 == e for e in range(2)], 1).astype(f4)
    second = np.where(row % 32 == 1, -1.0, 0.0).astype(f4)[:, None]
    causal = np.where(np.arange(S)[None, :] <= np.arange(S)[:, None], 0.0, HIDDEN).astype(f4)
    arrays = {
        "xT": host(x).reshape(TOK, D).T, "x": host(x).reshape(TOK, D), "ctxT": host(ctx_2048).reshape(TOK, D).T,
        "wqkvT": host(L0_attn_w_qkv).T, "woutT": host(L0_attn_w_out).T, "Wq": host(L0_xattn_Wq),
        "Wk": host(L0_xattn_Wk), "Wv": host(L0_xattn_Wv), "Wo": host(L0_xattn_Wo),
        "WupT": np.stack([host(L0_ffn_W0a).T, host(L0_ffn_W1a).T]),
        "WdownT": np.stack([host(L0_ffn_W0b).T, host(L0_ffn_W1b).T]),
        "bias_rows": np.stack([b_qkv, np.concatenate([bk, b_out]), np.concatenate([bv, b0b]),
                               np.concatenate([b1b, b1b, b1b])]),
        "columns": np.concatenate([
            host(L0_xattn_bq).reshape(XH, XD).T, host(L0_ffn_b0a).reshape(FC, 128).T,
            host(L0_ffn_b1a).reshape(FC, 128).T, host(L0_xattn_qn_w)[:, None],
            host(L0_xattn_kn_w)[:, None], head, second], 1),
        "gate_w": host(L0_ffn_Wg), "mask": host(mask_1xSxS2_ff0)[0], "causal": causal,
        "identity": np.eye(128, dtype=f4),
    }
    nc = bacc.Bacc("TRN2", target_bir_lowering=False, num_devices=1)
    sent, args = {}, []
    for name, a in arrays.items():
        a = np.ascontiguousarray(a)
        sent[f"in_{name}"] = a
        args.append(nc.dram_tensor(f"in_{name}", a.shape, mybir.dt.from_np(a.dtype), kind="ExternalInput").ap())
    out = nc.dram_tensor("out", (TOK, D), mybir.dt.float32, kind="ExternalOutput").ap()
    decoder(nc, *args, out)
    result = run_bass_kernel_spmd(nc, [sent], core_ids=[0])
    return result.results[0]["out"].reshape(NB, S, D)
```

```python
import concourse.bass as bass
from concourse import mybir
from contextlib import ExitStack

D = 256
NB, S = 16, 64
TOK = NB * S
T = 256
NT = TOK // T
NC = TOK // 128
KC = D // 128
SH, SD = 16, 16
XH, XKV, XD = 16, 4, 128
GH = XH // XKV
NX = XKV * NT
NA = NT * 4
FF = 512
FC = FF // 128
NBANK = 7
NSTAGE = 2
SLOT = 1024
SPLITS = ((0, 0), (0, 1), (1, 0))
LN_EPS, RMS_EPS = 1e-5, 1e-6
HIDDEN = -1.0e30

C_BQ, C_BUP, C_QN, C_KN, C_HEAD, C_SECOND, NCOLS = 0, 16, 24, 25, 26, 28, 29
RW = 768
R_QKV, R_OUT, R_K, R_V, R_DOWN = (0, 0), (1, 512), (1, 0), (2, 0), ((2, 512), (3, 0))

ITEMS = ([("x", 0), ("qk", 0), ("v", 0), ("ctx", 0), ("wk", 0), ("wv", 0), ("aout", 0)]
         + [("x", 1), ("ctx", 1), ("x", 2), ("ctx", 2), ("x", 3), ("ctx", 3)]
         + [("xq", 0), ("xo", 0), ("xq", 1), ("xo", 1)]
         + [("up", 0), ("up", 1), ("down", 0), ("down", 1)]
         + [("xq", 2), ("xo", 2), ("xq", 3), ("xo", 3)])
LOW_ON_POOL = [i % 2 == 1 and i > 6 for i in range(len(ITEMS))]


def block_of(b, i):
    return (b % 2) * 4 + (b // 2) * 2 + i


def schedule():
    out, items = [], iter(range(len(ITEMS)))

    def add(*stages):
        out.extend(stages)

    def load(n=1):
        add(*(("load", next(items)) for _ in range(n)))

    load(2)
    add(("a_project", 0))
    load(1)
    add(("a_read", 0), ("v_copies", 0))
    loads = {0: 2, 1: 2, 2: 1, 3: 1, 5: 1, 6: 1, 8: 1, 9: 1, 10: 1, 12: 1, 13: 1, 14: 1}
    for n in range(NA + 2):
        if n < NA:
            add(("a_scores", n), ("soft_a", n), ("soft_m", n), ("soft_shift", n))
        if n % 4 == 0 and 4 < n:
            add(("norm_turn", (0, n // 4 - 2)))
        if n >= 2:
            m, t = n - 2, (n - 2) // 4
            add(("a_values", m))
            if m % 4 == 3:
                add(("a_split", t))
                if t + 1 < NT:
                    add(("v_copies", t + 1))
                if t + 1 == NT:
                    add(("x_query", 0), ("q_parts", (0, 0)), ("q_parts", (0, 1)))
        if n % 4 == 3:
            if n < NA - 1:
                add(("a_read", n // 4 + 1))
        if n % 2 == 1 and n >= 3:
            add(("k_turn", n // 2 - 1))
        if n % 2 == 1 and n // 2 < NC:
            add(("k_project", n // 2))
        if n % 2 == 0 and 0 < n:
            add(("v_project", n // 2 - 1))
        if n % 4 == 1 and n > 4:
            add(("a_out", n // 4 - 1))
        if n < NA:
            add(("soft_exp", n), ("soft_b", n), ("soft_scale", n))
        if n % 2 == 1 and n >= 3:
            add(("k_turn_read", n // 2 - 1))
        if n % 2 == 1 and n // 2 < NC:
            add(("k_read", n // 2))
        if n % 2 == 0 and 0 < n:
            add(("v_read", n // 2 - 1))
        if n % 4 == 1 and n > 4:
            add(("norm", (0, n // 4 - 1)))
        if 1 <= n <= NA:
            add(("turn", n - 1), ("turn_read", n - 1))
        if n < NA:
            add(("soft_hi", n), ("soft_c", n))
        if n % 4 == 1 and n > 4:
            add(("norm_end", (0, n // 4 - 1)))
        load(loads.get(n, 0))
        if n % 4 == 2 and n // 4 + 1 < NT:
            add(("a_project", n // 4 + 1))
    add(("sq_parts", 0), ("x_query", 1), ("x_squares", 0), ("q_parts", (1, 0)), ("q_pow", 0),
        ("q_parts", (1, 1)), ("sq_parts", 1), ("norm_turn", (0, NT - 1)))
    loads = {0: 1, 1: 1, 2: 1, 3: 1, 4: 1, 5: 1, 8: 1, 9: 1}
    for s in range(NX + 2):
        w = s + 2
        last = s - 1 - (NX - NT)
        ffn = last - 1
        if s < NX:
            add(("x_scores", s), ("soft_a", NA + s), ("soft_mask", NA + s))
        if 0 <= ffn:
            add(("norm_turn", (1, ffn)))
        if 1 <= s <= NX:
            add(("x_values", s - 1))
        if s + 1 < NX:
            add(("x_squares", s + 1))
        if 1 <= s <= NX:
            add(("x_values_read", (s - 1, 0)))
        if s < NX:
            add(("soft_m", NA + s), ("soft_shift", NA + s))
        if s + 1 < NX:
            add(("q_pow", s + 1))
        if 1 <= s <= NX:
            add(("x_values_read", (s - 1, 1)))
        if w < NX:
            add(("x_query", w), ("q_parts", (w, 0)))
        if 0 <= ffn:
            add(("gate", ffn), ("f_up", (ffn, 0, 0)))
        if s < NX:
            add(("soft_exp", NA + s), ("soft_b", NA + s), ("soft_scale", NA + s))
        if 1 <= s <= NX:
            add(("x_out", s - 1))
        if w < NX:
            add(("q_parts", (w, 1)))
        if 0 <= ffn:
            add(("f_up", (ffn, 0, 1)))
        if 1 <= s <= NX:
            add(("x_add", s - 1))
        if 0 <= last < NT:
            add(("norm", (1, last)))
        if s < NX:
            add(("soft_hi", NA + s), ("soft_c", NA + s))
        if 0 <= ffn:
            add(("f_up", (ffn, 1, 0)))
        if 0 <= last < NT:
            add(("norm_end", (1, last)))
        if w < NX:
            add(("sq_parts", w))
        load(loads.get(s, 0))
        if s < NX:
            add(("turn", NA + s), ("turn_read", NA + s))
        if 0 <= ffn:
            add(("f_up", (ffn, 1, 1)), ("f_down", (ffn, 0)), ("f_down", (ffn, 1)), ("norm", (2, ffn)),
                ("norm_end", (2, ffn)), ("store", ffn))
    assert next(items, None) is None
    return out


STAGE_JOBS = {
    "a_project": ("dve",) * 3, "a_scores": ("dve",), "turn": ("act",), "a_out": ("dve",),
    "norm_turn": ("dve",), "k_project": ("dve",), "v_project": ("dve",), "k_turn": ("dve",),
    "x_query": ("dve",) * 2, "x_squares": ("dve",), "x_scores": ("dve",), "x_values": ("dve",) * 2,
    "x_out": ("dve",), "f_up": ("act",), "f_down": ("dve",),
}
READ_IN = {"a_read": "a_project", "turn_read": "turn", "k_turn_read": "k_turn", "k_read": "k_project",
           "v_read": "v_project", "x_add": "x_out"}
READ_ONE = {"q_parts": "x_query", "x_values_read": "x_values"}
SCHEDULE = schedule()


def number_jobs():
    first, engines = {}, []
    for name, k in SCHEDULE:
        jobs = STAGE_JOBS.get(name, ())
        if jobs:
            first[name, k] = len(engines)
            engines += jobs
    ends, count = {}, {"dve": 0, "act": 0}
    elsewhere = ("a_scores", "x_scores", *READ_IN.values(), *READ_ONE.values())
    for name, k in SCHEDULE:
        if name == "soft_a":
            jobs = [first["a_scores", k] if k < NA else first["x_scores", k - NA]]
        elif name in READ_ONE:
            jobs = [first[READ_ONE[name], k[0]] + k[1]]
        elif name in elsewhere:
            jobs = []
        else:
            filler = READ_IN.get(name, name)
            jobs = [first[filler, k] + i for i in range(len(STAGE_JOBS.get(filler, ())))]
        for job in jobs:
            count[engines[job]] += 1
            ends[job] = (engines[job], count[engines[job]])
    return first, ends


FIRST_JOB, JOB_ENDS = number_jobs()


def decoder(nc, xT, x, ctxT, wqkvT, woutT, Wq, Wk, Wv, Wo, WupT, WdownT, bias_rows, columns, gate_w, mask,
            causal, identity, out):
    f32, f32r, f16, bf16 = mybir.dt.float32, mybir.dt.float32r, mybir.dt.float16, mybir.dt.bfloat16
    ALU, ACT, AX = mybir.AluOpType, mybir.ActivationFunctionType, mybir.AxisListType

    ctx = ExitStack()
    with ctx:
        def sb(name, shape, dt):
            return ctx.enter_context(nc.sbuf_tensor(name, shape, dt))

        def sem(name):
            return ctx.enter_context(nc.semaphore(name))

        stage = sb("stage", [128, NSTAGE, SLOT], f32)
        acts = sb("acts", [128, 2, KC, TOK], f32r)
        resid = sb("resid", [128, NC, D], f32)
        w_kv = sb("w_kv", [128, 2, 2, 1024], f32r)
        w_a = sb("w_a", [128, 4096], f32r)
        w_xq = sb("w_xq", [128, 2, 2, 1024], f32r)
        w_xo = sb("w_xo", [128, 2, 2, 1024], f32r)
        parts = sb("parts", [128, 2, 1024], f32r)
        rows = sb("rows", [128, RW], f32r)
        ones = sb("ones", [128, T], f32r)
        keys = sb("keys", [128, 2, XKV, TOK], f16)
        values = sb("values", [128, NB, 2, XKV * XD], f16)
        queries = sb("queries", [128, 2, 2, 1024], f16)
        a_values_sb = queries[:, :, :, :].rearrange("p a b c -> p (a b c)")\
            .rearrange("p (b l n) -> p b l n", b=4, l=2)
        a_q = sb("a_q", [128, 2, 8, 128], f16)
        a_k = sb("a_k", [128, 2, 512], f16)
        v_spread = sb("v_spread", [128, 2, 2, 512], f16)
        v_parts = sb("v_parts", [128, 2, 512], f16)
        k_raw = sb("k_raw", [128, 512], f32)
        k_sq = sb("k_sq", [128, 512], f32)
        sq = v_spread[:, :, :, :].rearrange("p j l n -> p (j l n)").bitcast(f32)
        sq_hi = a_q[:, 0, :, :].rearrange("p e n -> p (e n)").bitcast(bf16)
        sq_lo = a_q[:, 1, :, :].rearrange("p e n -> p (e n)")
        scores = sb("scores", [128, 2, 512], f32)
        probs = sb("probs", [128, 2, 8, 128], f16)
        probsT = sb("probsT", [128, 2, 8, 128], f16)
        attn = sb("attn", [128, 2, 1024], f32r)
        hidden = k_sq, k_raw
        cols = sb("cols", [128, NCOLS], f32)
        key_scale = sb("key_scale", [128, 1], f32)
        gate_sb = sb("gate_sb", [128, 2, D], f32)
        gate_junk = sb("gate_junk", [128, D], bf16)
        logits = sb("logits", [128, 2, 2], f32)
        routed = sb("routed", [128, 2, 2], f32)
        mask_sb = sb("mask_sb", [128, S], f32)
        causal_sb = sb("causal_sb", [128, S], f32)
        ident = sb("ident", [128, 128], f32)
        ident16 = sb("ident16", [128, 128], f16)
        one16 = sb("one16", [128, 1], f16)
        onebf = sb("onebf", [128, 1], bf16)
        minus_half = sb("minus_half", [128, 8], f32)
        peak = sb("peak", [128, 8], f32)
        total = sb("total", [128, 8], f32)
        inverse = sb("inverse", [128, 8], f32)
        q_ms = sb("q_ms", [128, 8], f32)
        q_rms = sb("q_rms", [128, 2, 8], f32)
        k_ms = sb("k_ms", [128, XKV], f32)
        k_rms = sb("k_rms", [128, XKV], f32)
        stats = sb("stats", [128, 2, 6], f32)
        moments = sb("moments", [128, 2, 2], f32)
        ln_var = sb("ln_var", [128, 2], f32)
        ln_rstd = sb("ln_rstd", [128, 2], f32)
        gather = ctx.enter_context(nc.psum_tensor("gather", [128, 512], f32))
        banks = [ctx.enter_context(nc.psum_tensor(f"bank{i}", [128, 512], f32)) for i in range(NBANK)]

        w_qkv = w_a[:, 0:3072].rearrange("p (l k n) -> p l k n", l=2, k=KC)
        w_aout = w_a[:, 3072:4096].rearrange("p (l k n) -> p l k n", l=2, k=KC)
        w_down = w_a[:, :].rearrange("p (e l f n) -> p e l f n", e=2, l=2, f=FC)
        w_up = w_kv[:, :, :, :].rearrange("p e l (k n) -> p e l k n", k=KC)
        w_xq_v = w_xq[:, :, :, :].rearrange("p g l (k n) -> p g l k n", k=KC)
        w_xo_v = w_xo[:, :, :, :].rearrange("p g l (h n) -> p g l h n", h=GH)
        ctx_parts = parts[:, :, :].rearrange("p s (l k n) -> p s l k n", l=2, k=KC)
        hid_room = parts, w_xq[:, 0, :, :]
        hid_parts = [a[:, :, :].rearrange("p l (f n) -> p l f n", f=FC) for a in hid_room]
        attn_x = attn[:, :, :].rearrange("p l (h n) -> p l h n", h=GH)

        filled = sem("filled")
        freed = {"dve": sem("freed_by_dve"), "act": sem("freed_by_act")}
        s_const = sem("s_const")
        s_rows_in = sem("s_rows_in")
        s_resid = [sem(f"s_resid{t}") for t in range(NT)]
        s_staged = [sem(f"s_staged{i}") for i in range(NSTAGE)]
        s_high = sem("s_high")
        s_low = {False: sem("s_low_dve"), True: sem("s_low_pool")}
        s_zero = sem("s_zero")
        s_made = sem("s_made")
        s_pool_made = sem("s_pool_made")
        s_rows = sem("s_rows")
        s_aq_hi, s_ak_hi, s_av_hi = sem("s_aq_hi"), sem("s_ak_hi"), sem("s_av_hi")
        s_v_hi, s_key_hi, s_attn_hi, s_acts_hi = sem("s_v_hi"), sem("s_key_hi"), sem("s_attn_hi"), sem("s_acts_hi")
        s_q_hi = sem("s_q_hi")
        s_av_copied, s_v_copied = sem("s_av_copied"), sem("s_v_copied")
        s_k_read = sem("s_k_read")
        s_k_sum, s_k_ms, s_k_rms, s_k_normed = sem("s_k_sum"), sem("s_k_ms"), sem("s_k_rms"), sem("s_k_normed")
        s_masked, s_peak, s_shifted, s_exp = sem("s_masked"), sem("s_peak"), sem("s_shifted"), sem("s_exp")
        s_total, s_inverse, s_prob = sem("s_total"), sem("s_inverse"), sem("s_prob")
        s_prob_hi, s_probs = sem("s_prob_hi"), sem("s_probs")
        s_values = sem("s_values")
        s_gather_read = sem("s_gather_read")
        s_sq_hi, s_sq = sem("s_sq_hi"), sem("s_sq")
        s_q_ms, s_q_rms = sem("s_q_ms"), sem("s_q_rms")
        s_stats, s_moments, s_var, s_rstd, s_normed = (
            sem("s_stats"), sem("s_moments"), sem("s_var"), sem("s_rstd"), sem("s_normed"))
        s_logits, s_route0, s_route = sem("s_logits"), sem("s_route0"), sem("s_route")
        s_hid_hi, s_hid = sem("s_hid_hi"), sem("s_hid")
        s_stored = sem("s_stored")

        block = ctx.enter_context(nc.Block())

        def bank_of(job):
            return banks[job % NBANK]

        def job_of(name, k, i=0):
            return FIRST_JOB[name, k] + i

        def wait_filled(eng, job):
            eng.wait_ge(filled, job + 1)

        def wait_bank(eng, job):
            if job >= NBANK:
                engine, count = JOB_ENDS[job - NBANK]
                eng.wait_ge(freed[engine], count)

        def wait_read(eng, job):
            engine, count = JOB_ENDS[job]
            eng.wait_ge(freed[engine], count)

        def wait_item(eng, kind, k=0):
            i = ITEMS.index((kind, k))
            on_pool = LOW_ON_POOL[i]
            eng.wait_ge(s_low[on_pool], sum(LOW_ON_POOL[j] == on_pool for j in range(i + 1)))

        NORMS = [k for name, k in SCHEDULE if name == "norm"]
        TURNS = [k for name, k in SCHEDULE if name == "norm_turn"]
        UPS = [k for name, k in SCHEDULE if name == "f_up"]

        def norm_no(k):
            return NORMS.index(k)

        def item_parts(i):
            kind, k = ITEMS[i]
            if kind == "x":
                return [acts[:, l, :, k * T:(k + 1) * T] for l in range(2)]
            if kind == "qk":
                return [w_qkv[:, l, :, 0:512] for l in range(2)]
            if kind == "v":
                return [w_qkv[:, l, :, 512:768] for l in range(2)]
            if kind == "ctx":
                return [ctx_parts[:, k % 2, l, :, :] for l in range(2)]
            if kind in ("wk", "wv"):
                return [w_up[:, int(kind == "wv"), l, :, :] for l in range(2)]
            if kind == "aout":
                return [w_aout[:, l, :, :] for l in range(2)]
            if kind == "xq":
                return [w_xq_v[:, k % 2, l, :, :] for l in range(2)]
            if kind == "xo":
                return [w_xo_v[:, k % 2, l, :, :] for l in range(2)]
            if kind == "up":
                return [w_up[:, k, l, :, :] for l in range(2)]
            return [w_down[:, k, l, :, :] for l in range(2)]

        def item_source(i):
            kind, k = ITEMS[i]
            by_chunk = lambda a: a.rearrange("(k p) n -> p k n", p=128)
            if kind == "x":
                return by_chunk(xT)[:, :, k * T:(k + 1) * T]
            if kind == "ctx":
                return by_chunk(ctxT)[:, :, k * T:(k + 1) * T]
            if kind == "qk":
                return by_chunk(wqkvT)[:, :, 0:512]
            if kind == "v":
                return by_chunk(wqkvT)[:, :, 512:768]
            if kind == "xq":
                return by_chunk(Wq)[:, :, k * 512:(k + 1) * 512]
            if kind == "xo":
                return by_chunk(Wo)[:, k * GH:(k + 1) * GH, :]
            return by_chunk({"wk": Wk, "wv": Wv, "aout": woutT, "up": WupT[k], "down": WdownT[k]}[kind])

        def item_stage(i):
            shape = item_source(i).shape
            return stage[:, i % NSTAGE, 0:shape[1] * shape[2]].rearrange("p (k n) -> p k n", k=shape[1])

        def wait_item_room(eng, i):
            kind, k = ITEMS[i]
            if kind == "ctx" and k >= 2:
                wait_filled(eng, job_of("v_project", 2 * (k - 2) + 1))
            if kind == "xq" and k >= 2:
                wait_filled(eng, job_of("x_query", (k - 2) * NT + NT - 1, 1))
            if kind == "xo" and k >= 2:
                wait_filled(eng, job_of("x_out", (k - 2) * NT + NT - 1))
            if kind == "up":
                wait_filled(eng, job_of("v_project", NC - 1))
            if kind == "down":
                wait_filled(eng, job_of("a_out", NT - 1))

        def wait_unit_used(eng, n):
            if n >= NA:
                wait_filled(eng, job_of("x_values", n - NA, 1))
            else:
                eng.wait_ge(s_values, n + 1)

        def resid_of(t):
            return resid[:, 2 * t:2 * t + 2, :].rearrange("p j n -> p (j n)")

        def blocks(ap):
            return ap.rearrange("p (k n) -> p k n", n=S)

        def query_slots(ap, h):
            pair = ap[:, h // 2 * 512:(h // 2 + 1) * 512].rearrange("p (b n) -> p b n", b=4)
            return pair[:, :, h % 2 * S:(h % 2 + 1) * S]

        def each_block(ap):
            return ap.unsqueeze(2).to_broadcast([128, 8, S])

        def all_blocks(ap):
            return ap.unsqueeze(1).to_broadcast([128, 8, S])

        def prob_part(n, low, parity):
            at = S if low != bool(parity) else 0
            return probs[:, n % 2, 4 * parity:4 * parity + 4, at:at + S]

        @block.sync
        def _(sp):
            for i in range(len(ITEMS)):
                if i == 4:
                    for t in range(NT):
                        sp.dma_start(resid[:, 2 * t:2 * t + 2, :],
                                     x[t * T:(t + 1) * T, :].rearrange("(j p) n -> p j n", p=128))\
                            .then_inc(s_resid[t], 16)
                if i >= NSTAGE:
                    on_pool = LOW_ON_POOL[i - NSTAGE]
                    sp.wait_ge(s_low[on_pool], sum(LOW_ON_POOL[j] == on_pool for j in range(i - NSTAGE + 1)))
                sp.dma_start(item_stage(i), item_source(i)).then_inc(s_staged[i % NSTAGE], 16)
            for name, k in SCHEDULE:
                if name == "store":
                    sp.wait_ge(s_normed, norm_no((2, k)) + 1)
                    sp.dma_start(out[k * T:(k + 1) * T, :].rearrange("(j p) n -> p j n", p=128),
                                 resid[:, 2 * k:2 * k + 2, :]).then_inc(s_stored, 16)
            sp.wait_ge(s_stored, 16 * NT)

        @block.scalar
        def _(act):
            for dst, src in ((cols[:, :], columns), (ident[:, :], identity), (causal_sb[0:64, :], causal),
                             (causal_sb[64:128, :], causal), (mask_sb[0:64, :], mask),
                             (mask_sb[64:128, :], mask),
                             (gate_sb[:, :, :], gate_w.partition_broadcast(128))):
                act.dma_start(dst, src).then_inc(s_const, 16)
            act.wait_ge(s_zero, 1)
            for part in range(2):
                act.dma_start(scores[part:part + 97:32, 0:2, :].rearrange("p a n -> p (a n)")[:, 0:RW],
                              bias_rows).then_inc(s_rows_in, 16)
            act.wait_ge(s_const, 16 * 7)

            for name, k in SCHEDULE:
                if name == "load":
                    act.wait_ge(s_staged[k % NSTAGE], 16 * (k // NSTAGE + 1))
                    wait_item_room(act, k)
                    act.activation(item_parts(k)[0], item_stage(k), ACT.Copy).then_inc(s_high, 1)

                elif name == "a_read":
                    job = job_of("a_project", k)
                    wait_filled(act, job)
                    if k:
                        wait_filled(act, job_of("a_scores", 4 * k - 1))
                    for e in range(2):
                        act.activation(a_q[:, 0, :, e * S:(e + 1) * S], blocks(bank_of(job)[:, :]), ACT.Copy,
                                       scale=cols[:, C_HEAD + e:C_HEAD + e + 1]).then_inc(s_aq_hi, 1)
                    wait_filled(act, job + 1)
                    act.activation(a_k[:, 0, :], bank_of(job + 1)[:, :], ACT.Copy).then_inc(s_ak_hi, 1)
                    wait_filled(act, job + 2)
                    act.wait_ge(s_zero, 2)
                    if k:
                        act.wait_ge(s_av_copied, 16 * 8 * k)
                    bank = bank_of(job + 2)[:, :].rearrange("p (j i n) -> p j i n", j=2, n=2 * SD)
                    for e in range(2):
                        spread = v_spread[:, :, 0, :].rearrange("p j (i n) -> p j i n", n=4 * SD)
                        act.activation(spread[:, :, :, 3 * SD * e:3 * SD * e + SD],
                                       bank[:, :, :, SD * e:SD * e + SD], ACT.Copy).then_inc(s_av_hi, 1)

                elif name == "v_copies":
                    wait_read(act, job_of("a_project", k, 2))
                    act.wait_ge(s_made, 5)
                    if k:
                        wait_unit_used(act, 4 * k - 1)
                    for j in range(2):
                        for b, lo, hi in ((2 * j, 0, 64), (2 * j + 1, 64, 128)):
                            other = slice(64 - lo, 128 - lo)
                            act.dma_start(a_values_sb[lo:hi, b, :, :], v_spread[lo:hi, j, :, :])\
                                .then_inc(s_av_copied, 16)
                            act.dma_start(a_values_sb[other, b, 0, :], v_spread[lo:hi, j, 0, :])\
                                .then_inc(s_av_copied, 16)

                elif name == "k_read":
                    job = job_of("k_project", k)
                    wait_filled(act, job)
                    if k:
                        act.wait_ge(s_k_sum, k)
                    act.activation(k_sq[:, :], bank_of(job)[:, :], ACT.Square).then_inc(s_k_read, 1)

                elif name == "v_read":
                    job = job_of("v_project", k)
                    wait_filled(act, job)
                    if k:
                        act.wait_ge(s_v_copied, 16 * 4 * k)
                    act.activation(v_parts[:, 0, :], bank_of(job)[:, :], ACT.Copy).then_inc(s_v_hi, 1)

                elif name == "k_turn_read":
                    wait_read(act, job_of("v_project", k))
                    act.wait_ge(s_zero, 3)
                    for b, lo, hi in ((2 * k, 0, 64), (2 * k + 1, 64, 128)):
                        other = slice(64 - lo, 128 - lo)
                        act.dma_start(values[lo:hi, b, :, :], v_parts[lo:hi, :, :]).then_inc(s_v_copied, 16)
                        act.dma_start(values[other, b, 0, :], v_parts[lo:hi, 0, :]).then_inc(s_v_copied, 16)
                    job = job_of("k_turn", k)
                    wait_filled(act, job)
                    act.wait_ge(s_made, 8)
                    act.activation(keys[:, 0, :, k * 128:(k + 1) * 128],
                                   bank_of(job)[:, :].rearrange("p (g n) -> p g n", g=XKV), ACT.Copy,
                                   scale=key_scale[:, 0:1]).then_inc(s_key_hi, 1)

                elif name == "soft_exp":
                    act.wait_ge(s_shifted, k + 1)
                    act.activation(scores[:, k % 2, :], scores[:, k % 2, :], ACT.Exp).then_inc(s_exp, 1)

                elif name == "soft_hi":
                    act.wait_ge(s_prob, k + 1)
                    if k >= 2:
                        wait_filled(act, job_of("turn", k - 2))
                    for parity in range(2):
                        act.activation(prob_part(k, False, parity),
                                       blocks(scores[:, k % 2, :])[:, 4 * parity:4 * parity + 4, :],
                                       ACT.Copy).then_inc(s_prob_hi, 1)

                elif name == "turn_read":
                    job = job_of("turn", k)
                    wait_filled(act, job)
                    if k >= 2:
                        wait_unit_used(act, k - 2)
                    turned = act.activation(probsT[:, k % 2, :, :].rearrange("p k n -> p (k n)"),
                                            bank_of(job)[:, :].bitcast(f16), ACT.Copy)
                    turned.then_inc(freed["act"], 1)

                elif name == "a_split":
                    wait_unit_used(act, 4 * k + 3)
                    if k:
                        wait_filled(act, job_of("a_out", k - 1))
                    act.activation(attn[:, 0, 0:512], gather[:, :], ACT.Copy)\
                        .then_inc(s_attn_hi, 1)

                elif name == "norm_turn":
                    job = job_of(name, k)
                    wait_filled(act, job)
                    act.activation(acts[:, 0, :, k[1] * T:(k[1] + 1) * T],
                                   bank_of(job)[:, :].rearrange("p (k n) -> p k n", k=KC), ACT.Copy)\
                        .then_inc(s_acts_hi, 1)

                elif name == "q_parts":
                    u, pair = k
                    g, job = u // NT, job_of("x_query", u, pair)
                    if k == (0, 0):
                        wait_unit_used(act, NA - 1)
                    if u >= 2 and pair == 0:
                        wait_filled(act, job_of("x_scores", u - 2))
                    wait_filled(act, job)
                    if u and pair == 0:
                        act.wait_ge(s_sq, u)
                    for e in range(2):
                        h = 2 * pair + e
                        bias = cols[:, C_BQ + GH * g + h:C_BQ + GH * g + h + 1]
                        head = blocks(bank_of(job)[:, e * T:(e + 1) * T])
                        act.activation(query_slots(queries[:, u % 2, 0, :], h), head, ACT.Identity,
                                       bias=bias).then_inc(s_q_hi, 1)
                        act.activation(query_slots(sq, h), head, ACT.Square, bias=bias).then_inc(s_q_hi, 1)

                elif name == "sq_parts":
                    act.wait_ge(s_q_hi, 8 * (k + 1))
                    if k:
                        wait_filled(act, job_of("x_squares", k - 1))
                    act.activation(sq_hi, sq, ACT.Copy).then_inc(s_sq_hi, 1)

                elif name == "x_values_read":
                    u, parity = k
                    job = job_of("x_values", u, parity)
                    wait_filled(act, job)
                    if parity == 0:
                        wait_filled(act, job_of("x_out", u - 1) if u else job_of("a_out", NT - 1))
                    act.activation(
                        attn_x[:, 0, :, :].rearrange("p h (c r q) -> p r c h q", r=2, q=S)[:, parity],
                        bank_of(job)[:, :].rearrange("p (c h q) -> p c h q", h=GH, q=S), ACT.Copy)\
                        .then_inc(s_attn_hi, 1)

                elif name == "f_up":
                    t, e, f = k
                    job, n = job_of(name, k), UPS.index(k)
                    wait_filled(act, job)
                    if n >= 2:
                        act.wait_ge(s_hid, n - 1)
                    else:
                        wait_filled(act, job_of("k_turn", NC - 1))
                    for i in range(2):
                        c = C_BUP + FC * e + 2 * f + i
                        done = act.activation(hidden[n % 2][:, i * T:(i + 1) * T],
                                              bank_of(job)[:, i * T:(i + 1) * T],
                                              ACT.Relu if e else ACT.Gelu, bias=cols[:, c:c + 1])
                    done.then_inc(freed["act"], 1)

        @block.vector
        def _(dve):
            dve.memset(scores[:, :, :], 0.0).then_inc(s_zero, 1)
            dve.memset(v_spread[:, :, :, :], 0.0).then_inc(s_zero, 1)
            dve.memset(values[:, :, 1, :], 0.0).then_inc(s_zero, 1)
            dve.memset(ones[:, :].bitcast(f32), 1.0).then_inc(s_made, 1)
            dve.memset(minus_half[:, :], -0.5).then_inc(s_made, 1)
            dve.memset(one16[:, :], 1.0).then_inc(s_made, 1)
            dve.memset(onebf[:, :], 1.0).then_inc(s_made, 1)
            dve.memset(a_values_sb[:, :, 1, :], 0.0).then_inc(s_made, 1)
            dve.wait_ge(s_const, 16 * 7)
            dve.tensor_copy(ident16[:, :], ident[:, :]).then_inc(s_made, 1)
            dve.tensor_tensor(key_scale[:, :], cols[:, C_QN:C_QN + 1], cols[:, C_KN:C_KN + 1], ALU.mult)\
                .then_inc(s_made, 1)
            dve.wait_ge(s_made, 7)
            dve.tensor_scalar(key_scale[:, :], key_scale[:, :], float(XD) ** -0.5, None, ALU.mult)\
                .then_inc(s_made, 1)
            dve.wait_ge(s_rows_in, 32)
            raw = scores[:, :, :].rearrange("p a n -> p (a n)")[:, 0:RW]
            rounded = w_xq[:, 1, 1, 0:RW]
            dve.tensor_copy(rounded, raw).then_inc(s_rows, 1)
            dve.wait_ge(s_rows, 1)
            dve.scalar_tensor_tensor(rows[:, :], rounded.bitcast(f32), cols[:, C_SECOND:C_SECOND + 1], raw,
                                     ALU.mult, ALU.add).then_inc(s_rows, 1)

            for name, k in SCHEDULE:
                if name == "load":
                    if not LOW_ON_POOL[k]:
                        dve.wait_ge(s_high, k + 1)
                        dve.tensor_tensor(item_parts(k)[1], item_stage(k), item_parts(k)[0].bitcast(f32),
                                          ALU.subtract).then_inc(s_low[False], 1)

                elif name == "a_read":
                    job = job_of("a_project", k)
                    dve.wait_ge(s_aq_hi, 2 * (k + 1))
                    for e in range(2):
                        done = dve.scalar_tensor_tensor(
                            a_q[:, 1, :, e * S:(e + 1) * S], blocks(bank_of(job)[:, :]),
                            cols[:, C_HEAD + e:C_HEAD + e + 1], a_q[:, 0, :, e * S:(e + 1) * S],
                            ALU.mult, ALU.subtract)
                    done.then_inc(freed["dve"], 1)
                    dve.wait_ge(s_ak_hi, k + 1)
                    dve.tensor_tensor(a_k[:, 1, :], bank_of(job + 1)[:, :], a_k[:, 0, :], ALU.subtract)\
                        .then_inc(freed["dve"], 1)
                    dve.wait_ge(s_av_hi, 2 * (k + 1))
                    bank = bank_of(job + 2)[:, :].rearrange("p (j i n) -> p j i n", j=2, n=2 * SD)
                    spread = v_spread[:, :, :, :].rearrange("p j l (i n) -> p l j i n", n=4 * SD)
                    for e in range(2):
                        to = slice(3 * SD * e, 3 * SD * e + SD)
                        done = dve.tensor_tensor(spread[:, 1, :, :, to], bank[:, :, :, SD * e:SD * e + SD],
                                                 spread[:, 0, :, :, to], ALU.subtract)
                    done.then_inc(freed["dve"], 1)

                elif name == "k_read":
                    job = job_of("k_project", k)
                    dve.wait_ge(s_k_read, k + 1)
                    if k:
                        wait_filled(dve, job_of("k_turn", k - 1))
                    dve.tensor_copy(k_raw[:, :], bank_of(job)[:, :]).then_inc(freed["dve"], 1)
                    if k:
                        dve.wait_ge(s_k_rms, k)
                    dve.tensor_reduce(k_ms[:, :], k_sq[:, :].rearrange("p (g n) -> p g n", g=XKV), AX.X,
                                      ALU.add).then_inc(s_k_sum, 1)
                    dve.wait_ge(s_k_sum, k + 1)
                    dve.tensor_scalar(k_ms[:, :], k_ms[:, :], 1.0 / XD, RMS_EPS, ALU.mult, ALU.add)\
                        .then_inc(s_k_ms, 1)

                elif name == "v_read":
                    dve.wait_ge(s_v_hi, k + 1)
                    dve.tensor_tensor(v_parts[:, 1, :], bank_of(job_of("v_project", k))[:, :], v_parts[:, 0, :],
                                      ALU.subtract).then_inc(freed["dve"], 1)

                elif name == "k_turn_read":
                    dve.wait_ge(s_key_hi, k + 1)
                    at = slice(k * 128, (k + 1) * 128)
                    dve.scalar_tensor_tensor(
                        keys[:, 1, :, at], bank_of(job_of("k_turn", k))[:, :].rearrange("p (g n) -> p g n", g=XKV),
                        key_scale[:, 0:1], keys[:, 0, :, at], ALU.mult, ALU.subtract).then_inc(freed["dve"], 1)

                elif name == "soft_a":
                    if k >= 2:
                        dve.wait_ge(s_probs, k - 1)
                    if k < NA:
                        job = job_of("a_scores", k)
                        wait_filled(dve, job)
                        dve.scalar_tensor_tensor(blocks(scores[:, k % 2, :]), blocks(bank_of(job)[:, :]),
                                                 float(SD) ** -0.5, all_blocks(causal_sb[:, :]),
                                                 ALU.mult, ALU.add).then_inc(freed["dve"], 1)
                    else:
                        u = k - NA
                        job = job_of("x_scores", u)
                        wait_filled(dve, job)
                        dve.wait_ge(s_q_rms, u + 1)
                        dve.tensor_tensor(blocks(scores[:, k % 2, :]), blocks(bank_of(job)[:, :]),
                                          each_block(q_rms[:, u % 2, :]), ALU.mult).then_inc(freed["dve"], 1)

                elif name == "soft_m":
                    if k < NA:
                        wait_read(dve, job_of("a_scores", k))
                    else:
                        dve.wait_ge(s_masked, k - NA + 1)
                    if k:
                        dve.wait_ge(s_shifted, k)
                    dve.tensor_reduce(peak[:, :], blocks(scores[:, k % 2, :]), AX.X, ALU.max)\
                        .then_inc(s_peak, 1)

                elif name == "soft_b":
                    dve.wait_ge(s_exp, k + 1)
                    dve.tensor_reduce(total[:, :], blocks(scores[:, k % 2, :]), AX.X, ALU.add)\
                        .then_inc(s_total, 1)
                    dve.wait_ge(s_total, k + 1)
                    if k:
                        dve.wait_ge(s_prob, k)
                    dve.reciprocal(inverse[:, :], total[:, :]).then_inc(s_inverse, 1)

                elif name == "soft_c":
                    dve.wait_ge(s_prob_hi, 2 * (k + 1))
                    for parity in range(2):
                        done = dve.tensor_tensor(
                            prob_part(k, True, parity),
                            blocks(scores[:, k % 2, :])[:, 4 * parity:4 * parity + 4, :],
                            prob_part(k, False, parity), ALU.subtract)
                    done.then_inc(s_probs, 1)

                elif name == "a_split":
                    dve.wait_ge(s_attn_hi, k + 1)
                    dve.tensor_tensor(attn[:, 1, 0:512], gather[:, :], attn[:, 0, 0:512].bitcast(f32),
                                      ALU.subtract).then_inc(s_gather_read, 1)

                elif name == "a_out":
                    job = job_of(name, k)
                    wait_filled(dve, job)
                    dve.wait_ge(s_resid[k], 16)
                    dve.tensor_tensor(resid_of(k), bank_of(job)[:, :], resid_of(k), ALU.add)\
                        .then_inc(freed["dve"], 1)

                elif name == "norm":
                    w, t = k
                    wait_read(dve, (job_of("a_out", t), job_of("x_out", NX - NT + t) if w else 0,
                                    job_of("f_down", (t, 1)) if w else 0)[w])
                    n = norm_no(k)
                    if n:
                        dve.wait_ge(s_normed, n)
                    for j in range(2):
                        dve.bn_stats(stats[:, j, :], resid[:, 2 * t + j, :]).then_inc(s_stats, 1)
                    dve.wait_ge(s_stats, 2 * n + 2)
                    for j in range(2):
                        dve.bn_aggr(moments[:, j, :], stats[:, j, :]).then_inc(s_moments, 1)
                    dve.wait_ge(s_moments, 2 * n + 2)
                    dve.tensor_scalar(ln_var[:, :], moments[:, :, 1], LN_EPS, None, ALU.add).then_inc(s_var, 1)

                elif name == "norm_end":
                    t = k[1]
                    dve.wait_ge(s_rstd, norm_no(k) + 1)
                    for j in range(2):
                        done = dve.tensor_scalar(resid[:, 2 * t + j, :], resid[:, 2 * t + j, :],
                                                 moments[:, j, 0:1], ln_rstd[:, j:j + 1],
                                                 ALU.subtract, ALU.mult)
                    done.then_inc(s_normed, 1)

                elif name == "norm_turn":
                    wait_high = TURNS.index(k) + 1
                    dve.wait_ge(s_acts_hi, wait_high)
                    at = slice(k[1] * T, (k[1] + 1) * T)
                    dve.tensor_tensor(acts[:, 1, :, at],
                                      bank_of(job_of(name, k))[:, :].rearrange("p (k n) -> p k n", k=KC),
                                      acts[:, 0, :, at].bitcast(f32), ALU.subtract).then_inc(freed["dve"], 1)

                elif name == "q_parts":
                    u, pair = k
                    g, job = u // NT, job_of("x_query", u, pair)
                    dve.wait_ge(s_q_hi, 8 * u + 4 * pair + 4)
                    for e in range(2):
                        h = 2 * pair + e
                        done = dve.scalar_tensor_tensor(
                            query_slots(queries[:, u % 2, 1, :], h), blocks(bank_of(job)[:, e * T:(e + 1) * T]),
                            cols[:, C_BQ + GH * g + h:C_BQ + GH * g + h + 1],
                            query_slots(queries[:, u % 2, 0, :], h), ALU.add, ALU.subtract)
                    done.then_inc(freed["dve"], 1)

                elif name == "x_squares":
                    job = job_of(name, k)
                    wait_filled(dve, job)
                    if k:
                        dve.wait_ge(s_q_rms, k)
                    dve.tensor_scalar(q_ms[:, :], bank_of(job)[:, 0:8], 1.0 / XD, RMS_EPS, ALU.mult, ALU.add)\
                        .then_inc(freed["dve"], 1)

                elif name == "x_values_read":
                    u, parity = k
                    dve.wait_ge(s_attn_hi, NT + 2 * u + parity + 1)
                    at = lambda l: attn_x[:, l, :, :].rearrange(
                        "p h (c r q) -> p r c h q", r=2, q=S)[:, parity]
                    dve.tensor_tensor(
                        at(1), bank_of(job_of("x_values", u, parity))[:, :].rearrange(
                            "p (c h q) -> p c h q", h=GH, q=S),
                        at(0).bitcast(f32), ALU.subtract).then_inc(freed["dve"], 1)

                elif name == "x_add":
                    t = k % NT
                    job = job_of("x_out", k)
                    wait_filled(dve, job)
                    if k < NT:
                        dve.wait_ge(s_normed, norm_no((0, t)) + 1)
                    else:
                        wait_read(dve, job_of("x_out", k - NT))
                    dve.tensor_tensor(resid_of(t), bank_of(job)[:, :], resid_of(t), ALU.add)\
                        .then_inc(freed["dve"], 1)

                elif name == "gate":
                    dve.wait_ge(s_normed, norm_no((1, k)) + 1)
                    for j in range(2):
                        for e in range(2):
                            dve.tensor_tensor_reduce(gate_junk[:, :], resid[:, 2 * k + j, :], gate_sb[:, e, :],
                                                     1.0, 0.0, ALU.mult, ALU.add, logits[:, j, e:e + 1])\
                                .then_inc(s_logits, 1)
                            dve.wait_ge(s_logits, 4 * k + 2 * j + e + 1)
                    dve.tensor_tensor(routed[:, :, 0], logits[:, :, 0], logits[:, :, 1], ALU.is_ge)\
                        .then_inc(s_route0, 1)
                    dve.wait_ge(s_route0, k + 1)
                    dve.tensor_scalar(routed[:, :, 1], routed[:, :, 0], -1.0, 1.0, ALU.mult, ALU.add)\
                        .then_inc(s_route, 1)

                elif name == "f_up":
                    t, e, f = k
                    n = UPS.index(k)
                    dve.wait_ge(s_hid_hi, n + 1)
                    at = slice(f * 512, (f + 1) * 512)
                    dve.tensor_tensor(hid_room[e][:, 1, at], hidden[n % 2][:, :], hid_room[e][:, 0, at].bitcast(f32),
                                      ALU.subtract).then_inc(s_hid, 1)

                elif name == "f_down":
                    t, e = k
                    job = job_of(name, k)
                    wait_filled(dve, job)
                    dve.wait_ge(s_route, t + 1)
                    if e:
                        wait_read(dve, job_of(name, (t, 0)))
                    for j in range(2):
                        done = dve.scalar_tensor_tensor(resid[:, 2 * t + j, :], bank_of(job)[:, j * D:(j + 1) * D],
                                                        routed[:, j, e:e + 1], resid[:, 2 * t + j, :],
                                                        ALU.mult, ALU.add)
                    done.then_inc(freed["dve"], 1)

        @block.gpsimd
        def _(pool):
            for name, k in SCHEDULE:
                if name == "load":
                    if LOW_ON_POOL[k]:
                        pool.wait_ge(s_high, k + 1)
                        pool.tensor_tensor(item_parts(k)[1], item_stage(k), item_parts(k)[0].bitcast(f32),
                                           ALU.subtract).then_inc(s_low[True], 1)

                elif name == "k_read":
                    pool.wait_ge(s_k_ms, k + 1)
                    pool.wait_ge(s_made, 2)
                    pool.tensor_tensor(k_rms[:, :], k_ms[:, :], minus_half[:, 0:XKV], ALU.pow)\
                        .then_inc(s_k_rms, 1)
                    pool.wait_ge(s_k_rms, k + 1)
                    by_head = k_raw[:, :].rearrange("p (g n) -> p g n", g=XKV)
                    pool.tensor_tensor(by_head, by_head, k_rms[:, :].unsqueeze(2).to_broadcast([128, XKV, XD]),
                                       ALU.mult).then_inc(s_k_normed, 1)

                elif name == "soft_mask":
                    wait_read(pool, job_of("x_scores", k - NA))
                    at = blocks(scores[:, k % 2, :])
                    pool.tensor_tensor(at, at, all_blocks(mask_sb[:, :]), ALU.add).then_inc(s_masked, 1)

                elif name == "soft_shift":
                    pool.wait_ge(s_peak, k + 1)
                    at = blocks(scores[:, k % 2, :])
                    pool.tensor_tensor(at, at, each_block(peak[:, :]), ALU.subtract).then_inc(s_shifted, 1)

                elif name == "soft_scale":
                    pool.wait_ge(s_inverse, k + 1)
                    at = blocks(scores[:, k % 2, :])
                    pool.tensor_tensor(at, at, each_block(inverse[:, :]), ALU.mult).then_inc(s_prob, 1)

                elif name == "norm":
                    pool.wait_ge(s_var, norm_no(k) + 1)
                    pool.tensor_tensor(ln_rstd[:, :], ln_var[:, :], minus_half[:, 0:2], ALU.pow)\
                        .then_inc(s_rstd, 1)

                elif name == "sq_parts":
                    pool.wait_ge(s_sq_hi, k + 1)
                    pool.tensor_tensor(sq_lo, sq, sq_hi, ALU.subtract).then_inc(s_sq, 1)

                elif name == "q_pow":
                    wait_read(pool, job_of("x_squares", k))
                    if k >= 2:
                        wait_read(pool, job_of("x_scores", k - 2))
                    pool.tensor_tensor(q_rms[:, k % 2, :], q_ms[:, :], minus_half[:, :], ALU.pow)\
                        .then_inc(s_q_rms, 1)

                elif name == "f_up":
                    t, e, f = k
                    n = UPS.index(k)
                    wait_read(pool, job_of(name, k))
                    if t:
                        wait_filled(pool, job_of("f_down", (t - 1, e)))
                    elif e:
                        wait_filled(pool, job_of("x_query", NX - NT - 1, 1))
                    else:
                        wait_filled(pool, job_of("v_project", NC - 1))
                    pool.tensor_scalar(hid_room[e][:, 0, f * 512:(f + 1) * 512], hidden[n % 2][:, :], 1.0, 0.0,
                                       ALU.mult, ALU.add).then_inc(s_hid_hi, 1)

        @block.tensor
        def _(pe):
            def bias(out_ap, row, width, tokens_first, col=0):
                group, first = row
                at = slice(32 * group, 32 * group + 2)
                bias_row = rows[at, first + col:first + col + width]
                if tokens_first:
                    pe.matmul(out_ap, ones[at, 0:128], bias_row, start=True, stop=False)
                else:
                    pe.matmul(out_ap, bias_row, ones[at, 0:T], start=True, stop=False)

            def product(out_ap, still, moving, chunks, start):
                for c in range(chunks):
                    for i, (a, b) in enumerate(SPLITS):
                        done = pe.matmul(out_ap, still(a, c), moving(b, c), start=start and c == 0 and i == 0,
                                         stop=c == chunks - 1 and i == len(SPLITS) - 1)
                return done

            pe.wait_ge(s_made, 8)
            pe.wait_ge(s_rows, 2)
            for name, k in SCHEDULE:
                if name == "a_project":
                    wait_item(pe, "x", k)
                    wait_item(pe, "qk")
                    tile = slice(k * T, (k + 1) * T)
                    for which in range(2):
                        job = job_of(name, k, which)
                        wait_bank(pe, job)
                        for c in range(2):
                            to, col = bank_of(job)[:, c * T:(c + 1) * T], which * D + c * 128
                            bias(to, R_QKV, 128, False, col)
                            done = product(to, lambda l, q: w_qkv[:, l, q, col:col + 128],
                                           lambda l, q: acts[:, l, q, tile], KC, False)
                        done.then_inc(filled, 1)
                    wait_item(pe, "v")
                    job = job_of(name, k, 2)
                    wait_bank(pe, job)
                    for j in range(2):
                        to, tok = bank_of(job)[:, j * D:(j + 1) * D], k * T + j * 128
                        bias(to, R_QKV, D, True, 2 * D)
                        done = product(to, lambda l, q: acts[:, l, q, tok:tok + 128],
                                       lambda l, q: w_qkv[:, l, q, 2 * D:3 * D], KC, False)
                    done.then_inc(filled, 1)

                elif name == "a_scores":
                    job = job_of(name, k)
                    wait_read(pe, job_of("a_project", k // 4, 1))
                    wait_bank(pe, job)
                    rows32 = slice(32 * (k % 4), 32 * (k % 4) + 32)
                    for b in range(4):
                        for i in range(2):
                            tok = slice(i * T + b * S, i * T + (b + 1) * S)
                            at = block_of(b, i)
                            done = product(bank_of(job)[:, at * S:(at + 1) * S],
                                           lambda l, _: a_q[rows32, l, 4 * i + b, :],
                                           lambda l, _: a_k[rows32, l, tok], 1, True)
                    done.then_inc(filled, 1)

                elif name == "turn":
                    job = job_of(name, k)
                    pe.wait_ge(s_probs, k + 1)
                    wait_bank(pe, job)
                    turned = bank_of(job)[:, :].bitcast(f16)
                    for at in range(8):
                        done = pe.transpose(turned[:, at * 128:(at + 1) * 128], probs[:, k % 2, at, :],
                                            ident16[:, :])
                    done.then_inc(filled, 1)

                elif name == "a_values":
                    t, r = k // 4, k % 4
                    wait_read(pe, job_of("turn", k))
                    if r == 0:
                        pe.wait_ge(s_av_copied, 16 * 8 * (t + 1))
                        if t:
                            pe.wait_ge(s_gather_read, t)
                    for b in range(4):
                        for i in range(2):
                            to = gather[32 * r:32 * r + 32, i * T + b * S:i * T + (b + 1) * S]
                            for e in range(2):
                                at = (4 * i + r) * 4 * SD + e * 2 * SD
                                for l in range(2):
                                    done = pe.matmul(to, a_values_sb[:, b, l, at:at + 2 * SD],
                                                     probsT[:, k % 2, block_of(b, i), e * S:(e + 1) * S],
                                                     start=e == 0 and l == 0, stop=e == 1 and l == 1)
                    done.then_inc(s_values, 1)

                elif name == "a_out":
                    job = job_of(name, k)
                    wait_item(pe, "aout")
                    pe.wait_ge(s_gather_read, k + 1)
                    wait_bank(pe, job)
                    for j in range(2):
                        to = bank_of(job)[:, j * D:(j + 1) * D]
                        bias(to, R_OUT, D, True)
                        done = product(to, lambda l, c: attn[:, l, c * T + j * 128:c * T + (j + 1) * 128],
                                       lambda l, c: w_aout[:, l, c, :], KC, False)
                    done.then_inc(filled, 1)

                elif name == "norm_turn":
                    job = job_of(name, k)
                    pe.wait_ge(s_normed, norm_no(k) + 1)
                    wait_bank(pe, job)
                    for c in range(KC):
                        for j in range(2):
                            done = pe.transpose(bank_of(job)[:, c * T + j * 128:c * T + (j + 1) * 128],
                                                resid[:, 2 * k[1] + j, c * 128:(c + 1) * 128], ident[:, :])
                    done.then_inc(filled, 1)

                elif name in ("k_project", "v_project"):
                    which = int(name == "v_project")
                    slot, at = (k // 2) % 2, slice((k % 2) * 128, (k % 2) * 128 + 128)
                    wait_item(pe, "ctx", k // 2)
                    job = job_of(name, k)
                    wait_item(pe, ("wk", "wv")[which])
                    wait_bank(pe, job)
                    bias(bank_of(job)[:, :], (R_K, R_V)[which], 512, True)
                    product(bank_of(job)[:, :], lambda l, c: ctx_parts[:, slot, l, c, at],
                            lambda l, c: w_up[:, which, l, c, :], KC, False).then_inc(filled, 1)

                elif name == "k_turn":
                    job = job_of(name, k)
                    pe.wait_ge(s_k_normed, k + 1)
                    wait_bank(pe, job)
                    for g in range(XKV):
                        done = pe.transpose(bank_of(job)[:, g * 128:(g + 1) * 128],
                                            k_raw[:, g * 128:(g + 1) * 128], ident[:, :])
                    done.then_inc(filled, 1)

                elif name == "x_query":
                    g, t = k // NT, k % NT
                    wait_item(pe, "xq", g)
                    wait_read(pe, job_of("norm_turn", (0, t)))
                    for pair in range(2):
                        job = job_of(name, k, pair)
                        wait_bank(pe, job)
                        for e in range(2):
                            h = 2 * pair + e
                            done = product(bank_of(job)[:, e * T:(e + 1) * T],
                                           lambda l, c: w_xq_v[:, g % 2, l, c, h * 128:(h + 1) * 128],
                                           lambda l, c: acts[:, l, c, t * T:(t + 1) * T], KC, True)
                        done.then_inc(filled, 1)

                elif name == "x_squares":
                    job = job_of(name, k)
                    pe.wait_ge(s_sq, k + 1)
                    wait_bank(pe, job)
                    for b in range(4):
                        for i in range(2):
                            at = block_of(b, i)
                            slot = slice((4 * i + b) * 128, (4 * i + b + 1) * 128)
                            pe.matmul(bank_of(job)[:, at:at + 1], sq_hi[:, slot], onebf[:, :],
                                      start=True, stop=False)
                            done = pe.matmul(bank_of(job)[:, at:at + 1], sq_lo[:, slot], one16[:, :],
                                             start=False, stop=True)
                    done.then_inc(filled, 1)

                elif name == "x_scores":
                    g, t = k // NT, k % NT
                    job = job_of(name, k)
                    wait_read(pe, job_of("x_query", k, 1))
                    wait_read(pe, job_of("k_turn", 2 * t + 1))
                    wait_bank(pe, job)
                    for b in range(4):
                        for i in range(2):
                            at, tok = block_of(b, i), (4 * t + b) * S
                            slot = slice((4 * i + b) * 128, (4 * i + b + 1) * 128)
                            done = product(bank_of(job)[:, at * S:(at + 1) * S],
                                           lambda l, _: queries[:, k % 2, l, slot],
                                           lambda l, _: keys[:, l, g, tok:tok + S], 1, True)
                    done.then_inc(filled, 1)

                elif name == "x_values":
                    g, t = k // NT, k % NT
                    wait_read(pe, job_of("turn", NA + k))
                    pe.wait_ge(s_v_copied, 16 * 4 * (2 * t + 2))
                    for parity in range(2):
                        job = job_of(name, k, parity)
                        wait_bank(pe, job)
                        for c in range(2):
                            b = 2 * c + parity
                            at = block_of(b, 0)
                            for l in range(2):
                                done = pe.matmul(bank_of(job)[:, c * T:(c + 1) * T],
                                                 values[:, 4 * t + b, l, g * XD:(g + 1) * XD],
                                                 probsT[:, k % 2, at:at + 2, :], start=l == 0, stop=l == 1)
                        done.then_inc(filled, 1)

                elif name == "x_out":
                    g, t = k // NT, k % NT
                    job = job_of(name, k)
                    wait_item(pe, "xo", g)
                    wait_read(pe, job_of("x_values", k, 1))
                    wait_bank(pe, job)
                    for j in range(2):
                        done = product(bank_of(job)[:, j * D:(j + 1) * D],
                                       lambda l, h: attn_x[:, l, h, j * 128:(j + 1) * 128],
                                       lambda l, h: w_xo_v[:, g % 2, l, h, :], GH, True)
                    done.then_inc(filled, 1)

                elif name == "f_up":
                    t, e, f = k
                    job = job_of(name, k)
                    wait_item(pe, "up", e)
                    wait_read(pe, job_of("norm_turn", (1, t)))
                    wait_bank(pe, job)
                    for i in range(2):
                        col = (2 * f + i) * 128
                        done = product(bank_of(job)[:, i * T:(i + 1) * T],
                                       lambda l, c: w_up[:, e, l, c, col:col + 128],
                                       lambda l, c: acts[:, l, c, t * T:(t + 1) * T], KC, True)
                    done.then_inc(filled, 1)

                elif name == "f_down":
                    t, e = k
                    job = job_of(name, k)
                    wait_item(pe, "down", e)
                    pe.wait_ge(s_hid, UPS.index((t, e, 1)) + 1)
                    wait_bank(pe, job)
                    for j in range(2):
                        to = bank_of(job)[:, j * D:(j + 1) * D]
                        bias(to, R_DOWN[e], D, True)
                        done = product(to, lambda l, c: hid_parts[e][:, l, c, j * 128:(j + 1) * 128],
                                       lambda l, c: w_down[:, e, l, c, :], FC, False)
                    done.then_inc(filled, 1)


def kernel(x, ctx_2048, mask_1xSxS2_ff0, L0_attn_w_qkv, L0_attn_b_qkv, L0_attn_w_out, L0_attn_b_out,
           L0_xattn_Wq, L0_xattn_bq, L0_xattn_Wk, L0_xattn_bk, L0_xattn_Wv, L0_xattn_bv, L0_xattn_Wo,
           L0_xattn_qn_w, L0_xattn_kn_w, L0_ffn_Wg, L0_ffn_W0a, L0_ffn_b0a, L0_ffn_W0b, L0_ffn_b0b,
           L0_ffn_W1a, L0_ffn_b1a, L0_ffn_W1b, L0_ffn_b1b):
    import numpy as np
    import concourse.bacc as bacc
    from concourse.bass_utils import run_bass_kernel_spmd

    host = np.asarray
    b_qkv, b_out, bk, bv = host(L0_attn_b_qkv), host(L0_attn_b_out), host(L0_xattn_bk), host(L0_xattn_bv)
    b0b, b1b = host(L0_ffn_b0b), host(L0_ffn_b1b)
    f4 = np.float32
    row = np.arange(128)
    head = np.stack([(row // SD) % 2 == e for e in range(2)], 1).astype(f4)
    second = np.where(row % 32 == 1, -1.0, 0.0).astype(f4)[:, None]
    causal = np.where(np.arange(S)[None, :] <= np.arange(S)[:, None], 0.0, HIDDEN).astype(f4)
    arrays = {
        "xT": host(x).reshape(TOK, D).T, "x": host(x).reshape(TOK, D), "ctxT": host(ctx_2048).reshape(TOK, D).T,
        "wqkvT": host(L0_attn_w_qkv).T, "woutT": host(L0_attn_w_out).T, "Wq": host(L0_xattn_Wq),
        "Wk": host(L0_xattn_Wk), "Wv": host(L0_xattn_Wv), "Wo": host(L0_xattn_Wo),
        "WupT": np.stack([host(L0_ffn_W0a).T, host(L0_ffn_W1a).T]),
        "WdownT": np.stack([host(L0_ffn_W0b).T, host(L0_ffn_W1b).T]),
        "bias_rows": np.stack([b_qkv, np.concatenate([bk, b_out]), np.concatenate([bv, b0b]),
                               np.concatenate([b1b, b1b, b1b])]),
        "columns": np.concatenate([
            host(L0_xattn_bq).reshape(XH, XD).T, host(L0_ffn_b0a).reshape(FC, 128).T,
            host(L0_ffn_b1a).reshape(FC, 128).T, host(L0_xattn_qn_w)[:, None],
            host(L0_xattn_kn_w)[:, None], head, second], 1),
        "gate_w": host(L0_ffn_Wg), "mask": host(mask_1xSxS2_ff0)[0], "causal": causal,
        "identity": np.eye(128, dtype=f4),
    }
    nc = bacc.Bacc("TRN2", target_bir_lowering=False, num_devices=1)
    sent, args = {}, []
    for name, a in arrays.items():
        a = np.ascontiguousarray(a)
        sent[f"in_{name}"] = a
        args.append(nc.dram_tensor(f"in_{name}", a.shape, mybir.dt.from_np(a.dtype), kind="ExternalInput").ap())
    out = nc.dram_tensor("out", (TOK, D), mybir.dt.float32, kind="ExternalOutput").ap()
    decoder(nc, *args, out)
    result = run_bass_kernel_spmd(nc, [sent], core_ids=[0])
    return result.results[0]["out"].reshape(NB, S, D)
```

```python
import concourse.bass as bass
from concourse import mybir
from contextlib import ExitStack

D = 256
NB, S = 16, 64
TOK = NB * S
T = 256
NT = TOK // T
NC = TOK // 128
KC = D // 128
SD = 16
XH, XKV, XD = 16, 4, 128
GH = XH // XKV
NX = XKV * NT
NA = NT * 4
FF = 512
FC = FF // 128
NBANK = 7
DEEP = 3
NEARLY = 4
NSTAGE = 2
SLOT = 1024
SPLITS = ((0, 0), (0, 1), (1, 0))
LN_EPS, RMS_EPS = 1e-5, 1e-6
HIDDEN = -1.0e30

C_BQ, C_BUP, C_QN, C_KN, C_HEAD, C_SECOND, NCOLS = 0, 16, 24, 25, 26, 28, 29
RW = 768
R_QKV, R_OUT, R_K, R_V, R_DOWN = (0, 0), (1, 512), (1, 0), (2, 0), ((2, 512), (3, 0))

LOADS = (
    (("x", 0), -8.8794, "dve", -7.575),
    (("qk", 0), -1.6515, "pool", -1.8758),
    (("v", 0), -1.6108, "pool", -1.1347),
    (("ctx", 0), -0.2689, "pool", -0.0185),
    (("wk", 0), 0.2554, "dve", 0.713),
    (("wv", 0), 1.3299, "dve", 1.1762),
    (("aout", 0), 1.4023, "pool", 1.5838),
    (("x", 1), 1.9047, "dve", 2.056),
    (("ctx", 1), 4.3758, "pool", 5.2327),
    (("x", 2), 5.8976, "pool", 5.5422),
    (("ctx", 2), 6.9174, "pool", 7.0775),
    (("x", 3), 10.0703, "dve", 9.8387),
    (("xq", 0), 10.4704, "pool", 11.4507),
    (("xo", 0), 12.4393, "pool", 12.553),
    (("ctx", 3), 12.4802, "dve", 13.1685),
    (("xq", 1), 15.0656, "pool", 15.3045),
    (("xo", 1), 15.1187, "pool", 16.4907),
    (("up", 0), 17.0533, "pool", 18.2539),
    (("up", 1), 19.3056, "dve", 19.4398),
    (("down", 0), 20.1251, "dve", 20.4539),
    (("down", 1), 20.6707, "dve", 21.7485),
    (("xq", 2), 22.8277, "dve", 23.2583),
    (("xo", 2), 27.7707, "dve", 27.6284),
    (("xq", 3), 28.2977, "dve", 28.3177),
    (("xo", 3), 32.4393, "dve", 32.6889),
)
ITEMS = [item for item, *_ in LOADS]
LOW_ON_POOL = [engine == "pool" for _, _, engine, _ in LOADS]

TILES, CHUNKS, A_UNITS, X_UNITS = range(NT), range(NC), range(NA), range(NX)
X_SOFT = range(NA, NA + NX)
HALF0, HALF1 = [(u, 0) for u in X_UNITS], [(u, 1) for u in X_UNITS]
X_FIRST, X_REST = X_UNITS[:2], X_UNITS[2:]
HALF0_FIRST, HALF0_REST, HALF1_FIRST, HALF1_REST = HALF0[:2], HALF0[2:], HALF1[:2], HALF1[2:]
NORM0, NORM1, NORM2 = ([(w, t) for t in TILES] for w in range(3))
UP00, UP01, UP10, UP11 = ([(t, e, f) for t in TILES] for e in range(2) for f in range(2))
DOWN0, DOWN1 = ([(t, e) for t in TILES] for e in range(2))

PLAN = {
    "pe": (
        ("a_project", TILES, -1.035, 4),
        ("a_scores", A_UNITS, -0.128, 1),
        ("k_project", CHUNKS, 1.312, 2),
        ("turn", A_UNITS, 2.255, 1),
        ("v_project", CHUNKS, 3.186, 2),
        ("a_values", A_UNITS, 3.294, 1),
        ("k_turn", CHUNKS, 3.876, 2),
        ("a_out", TILES, 7.293, 4),
        ("norm_turn", NORM0, 8.384, 4),
        ("x_query", X_FIRST, 17.558, 1),
        ("x_squares", X_FIRST, 18.756, 1),
        ("x_scores", X_UNITS, 18.773, 1),
        ("x_query", X_REST, 19.557, 1),
        ("x_squares", X_REST, 20.746, 1),
        ("turn", X_SOFT, 21.617, 1),
        ("x_values", X_UNITS, 23.206, 1),
        ("x_out", X_UNITS, 24.281, 1),
        ("norm_turn", NORM1, 36.990, 1),
        ("f_up", UP00, 37.231, 1),
        ("f_up", UP01, 37.629, 1),
        ("f_up", UP10, 37.833, 1),
        ("f_up", UP11, 37.834, 1),
        ("f_down", DOWN0, 37.883, 1),
        ("f_down", DOWN1, 38.062, 1),
    ),
    "act": (
        ("a_read", TILES, -0.760, 4),
        ("soft_exp", A_UNITS, 1.077, 1),
        ("soft_hi", A_UNITS, 1.444, 1),
        ("k_read", CHUNKS, 2.248, 2),
        ("turn_read", A_UNITS, 2.359, 1),
        ("v_read", CHUNKS, 3.349, 2),
        ("k_turn_read", CHUNKS, 4.377, 2),
        ("a_split", TILES, 6.481, 4),
        ("norm_turn", NORM0, 8.666, 4),
        ("q_parts", HALF0_FIRST, 17.764, 1),
        ("q_parts", HALF1_FIRST, 18.001, 1),
        ("sq_parts", X_FIRST, 18.119, 1),
        ("q_parts", HALF0_REST, 20.028, 1),
        ("soft_exp", X_SOFT, 20.065, 1),
        ("q_parts", HALF1_REST, 20.156, 1),
        ("sq_parts", X_REST, 20.398, 1),
        ("soft_hi", X_SOFT, 21.313, 1),
        ("turn_read", X_SOFT, 22.493, 1),
        ("x_values_read", HALF0, 23.579, 1),
        ("x_values_read", HALF1, 23.872, 1),
        ("norm_turn", NORM1, 37.447, 1),
        ("f_up", UP00, 37.499, 1),
        ("f_up", UP01, 37.667, 1),
        ("f_up", UP10, 37.782, 1),
        ("f_up", UP11, 38.033, 1),
    ),
    "dve": (
        ("constants", [0], -1.247, 1),
        ("a_read", TILES, -0.845, 4),
        ("soft_a", A_UNITS, 0.252, 1),
        ("soft_m", A_UNITS, 0.546, 1),
        ("soft_b", A_UNITS, 1.080, 1),
        ("soft_c", A_UNITS, 1.616, 1),
        ("k_read", CHUNKS, 2.570, 2),
        ("v_read", CHUNKS, 3.839, 2),
        ("k_turn_read", CHUNKS, 4.632, 2),
        ("a_split", TILES, 6.706, 4),
        ("a_out", TILES, 7.822, 4),
        ("norm", NORM0, 7.924, 4),
        ("norm_end", NORM0, 8.188, 4),
        ("norm_turn", NORM0, 8.939, 4),
        ("q_parts", HALF0_FIRST, 18.055, 1),
        ("q_parts", HALF1_FIRST, 18.382, 1),
        ("x_squares", X_FIRST, 19.044, 1),
        ("soft_a", X_SOFT, 19.205, 1),
        ("soft_m", X_SOFT, 19.574, 1),
        ("q_parts", HALF0_REST, 20.125, 1),
        ("soft_b", X_SOFT, 20.163, 1),
        ("q_parts", HALF1_REST, 20.310, 1),
        ("x_squares", X_REST, 20.944, 1),
        ("soft_c", X_SOFT, 21.498, 1),
        ("x_values_read", HALF0, 23.756, 1),
        ("x_values_read", HALF1, 23.784, 1),
        ("x_add", X_UNITS, 24.535, 1),
        ("norm", NORM1, 36.664, 1),
        ("norm_end", NORM1, 36.766, 1),
        ("norm_turn", NORM1, 36.910, 1),
        ("gate", TILES, 36.928, 1),
        ("f_up", UP00, 37.425, 1),
        ("f_up", UP01, 37.683, 1),
        ("f_up", UP10, 37.758, 1),
        ("f_up", UP11, 37.773, 1),
        ("f_down", DOWN0, 37.837, 1),
        ("f_down", DOWN1, 38.027, 1),
        ("norm", NORM2, 38.146, 1),
        ("norm_end", NORM2, 38.496, 1),
    ),
    "pool": (
        ("soft_shift", A_UNITS, 0.467, 1),
        ("soft_scale", A_UNITS, 1.266, 1),
        ("k_read", CHUNKS, 2.589, 2),
        ("norm", NORM0, 8.084, 4),
        ("sq_parts", X_FIRST, 18.321, 1),
        ("q_pow", X_FIRST, 18.527, 1),
        ("soft_mask", X_SOFT, 19.311, 1),
        ("soft_shift", X_SOFT, 19.494, 1),
        ("sq_parts", X_REST, 20.463, 1),
        ("soft_scale", X_SOFT, 20.514, 1),
        ("q_pow", X_REST, 21.115, 1),
        ("norm", NORM1, 36.777, 1),
        ("f_up", UP00, 37.135, 1),
        ("f_up", UP01, 37.485, 1),
        ("f_up", UP10, 37.780, 1),
        ("f_up", UP11, 37.834, 1),
        ("norm", NORM2, 38.181, 1),
    ),
    "sp": (
        ("v_copies", TILES, 1.592, 4),
        ("kv_copies", CHUNKS, 3.387, 2),
        ("store", TILES, 35.737, 1),
    ),
}


def engine_order(engine):
    timed = [(first + step * i, name, key)
             for name, keys, first, step in PLAN[engine] for i, key in enumerate(keys)]
    if engine == "act":
        timed += [(at, "load", i) for i, (_, at, _, _) in enumerate(LOADS)]
    if engine == "sp":
        timed += [(-9 if i < NEARLY + NSTAGE else LOADS[i - NSTAGE][3] + 0.001, "load", i)
                  for i in range(len(LOADS))]
    if engine in ("dve", "pool"):
        timed += [(at, "load", i) for i, (_, _, on, at) in enumerate(LOADS) if on == engine]
    return [(name, key) for _, name, key in sorted(timed, key=lambda x: x[0])]


ORDER = {engine: engine_order(engine) for engine in PLAN}


def keys_of(name, engine):
    return [key for stage, key in ORDER[engine] if stage == name]


for stage in {row[0] for rows in PLAN.values() for row in rows}:
    assert len({tuple(keys_of(stage, engine)) for engine in PLAN} - {()}) == 1, stage
for engine in ("act", "dve", "pool"):
    for stage in ("load", "q_parts", "x_values_read"):
        assert keys_of(stage, engine) == sorted(keys_of(stage, engine))
assert [e for _, e in keys_of("f_down", "dve")] == [0, 1] * NT
assert [s for s in ORDER["dve"] if s[0] in ("norm", "norm_end")] == [
    (name, key) for key in keys_of("norm", "dve") for name in ("norm", "norm_end")]

STAGE_JOBS = {
    "a_project": ("dve",) * 3, "a_scores": ("dve",), "turn": ("act",), "a_out": ("dve",),
    "norm_turn": ("dve",), "k_project": ("act",), "v_project": ("dve",), "k_turn": ("dve",),
    "x_query": ("dve",) * 2, "x_squares": ("dve",), "x_scores": ("dve",), "x_values": ("dve",) * 2,
    "x_out": ("dve",), "f_up": ("act",), "f_down": ("dve",),
}
READS = {"a_read": "a_project", "turn_read": "turn", "k_turn_read": "k_turn", "k_read": "k_project",
         "v_read": "v_project", "x_add": "x_out"}
READS_ONE = {"q_parts": "x_query", "x_values_read": "x_values"}


def number_jobs():
    first, engines = {}, []
    for name, k in ORDER["pe"]:
        jobs = STAGE_JOBS.get(name, ())
        if jobs:
            first[name, k] = len(engines)
            engines += jobs
    ends = {}
    elsewhere = ("a_scores", "x_scores", *READS.values(), *READS_ONE.values())
    for engine in ("act", "dve"):
        count = 0
        for name, k in ORDER[engine]:
            if name == "soft_a":
                jobs = [first["a_scores", k] if k < NA else first["x_scores", k - NA]]
            elif name in READS_ONE:
                jobs = [first[READS_ONE[name], k[0]] + k[1]]
            elif name in elsewhere:
                jobs = []
            else:
                filler = READS.get(name, name)
                jobs = [first[filler, k] + i for i in range(len(STAGE_JOBS.get(filler, ())))]
            for job in jobs:
                if engines[job] == engine:
                    count += 1
                    ends[job] = (engine, count)
    return first, ends


FIRST_JOB, JOB_ENDS = number_jobs()


def block_of(b, i):
    return (b % 2) * 4 + (b // 2) * 2 + i


def decoder(nc, xT, x, ctxT, wqkvT, woutT, Wq, Wk, Wv, Wo, WupT, WdownT, bias_rows, columns, gate_w, mask,
            causal, identity, out):
    f32, f32r, f16, bf16 = mybir.dt.float32, mybir.dt.float32r, mybir.dt.float16, mybir.dt.bfloat16
    ALU, ACT, AX = mybir.AluOpType, mybir.ActivationFunctionType, mybir.AxisListType

    ctx = ExitStack()
    with ctx:
        def sb(name, shape, dt):
            return ctx.enter_context(nc.sbuf_tensor(name, shape, dt))

        def sem(name):
            return ctx.enter_context(nc.semaphore(name))

        stage = sb("stage", [128, NSTAGE, SLOT], f32)
        acts = sb("acts", [128, 2, KC, TOK], f32r)
        resid = sb("resid", [128, NC, D], f32)
        w_kv = sb("w_kv", [128, 2, 2, 1024], f32r)
        w_a = sb("w_a", [128, 4096], f32r)
        w_xq = sb("w_xq", [128, 2, 2, 1024], f32r)
        w_xo = sb("w_xo", [128, 2, 2, 1024], f32r)
        parts = sb("parts", [128, 2, 1024], f32r)
        rows = sb("rows", [128, RW], f32r)
        ones = sb("ones", [128, T], f32r)
        keys = sb("keys", [128, 2, XKV, TOK], f16)
        values_hi = sb("values_hi", [128, NB, XKV * XD], f16)
        values_lo = sb("values_lo", [128, NC, XKV * XD], f16)
        queries = sb("queries", [128, DEEP, 2, 1024], f16)
        a_values_hi = queries[:, DEEP - 1, :, :].rearrange("p a c -> p (a c)")\
            .rearrange("p (b n) -> p b n", b=4)
        a_q = sb("a_q", [128, 2, 8, 128], f16)
        a_k = sb("a_k", [128, 2, 512], f16)
        v_spread = sb("v_spread", [128, 2, 512], f16)
        a_values_lo = sb("a_values_lo", [128, 2, 2, 512], f16)
        v_parts = sb("v_parts", [128, 512], f16)
        k_raw = sb("k_raw", [128, 512], f32)
        k_sq = sb("k_sq", [128, 512], f32)
        sq = (a_q[:, :, :, :].rearrange("p l e n -> p (l e n)").bitcast(f32),
              a_values_lo[:, :, :, :].rearrange("p j l n -> p (j l n)").bitcast(f32))
        sq_hi = a_k[:, :, :].rearrange("p l n -> p (l n)").bitcast(bf16)
        sq_lo = v_spread[:, :, :].rearrange("p l n -> p (l n)")
        scores = sb("scores", [128, DEEP, 512], f32)
        probs = sb("probs", [128, DEEP, 8, 128], f16)
        probsT = sb("probsT", [128, DEEP, 8, 128], f16)
        attn = sb("attn", [128, 2, 1024], f32r)
        hidden = k_sq, k_raw
        cols = sb("cols", [128, NCOLS], f32)
        key_scale = sb("key_scale", [128, 1], f32)
        gate_sb = sb("gate_sb", [128, 2, D], f32)
        gate_junk = a_values_lo[:, 0, 0, 0:D].bitcast(bf16)
        logits = sb("logits", [128, NT, 2, 2], f32)
        routed = sb("routed", [128, NT, 2, 2], f32)
        mask_sb = sb("mask_sb", [128, S], f32)
        causal_sb = sb("causal_sb", [128, S], f32)
        ident = sb("ident", [128, 128], f32)
        ident16 = sb("ident16", [128, 128], f16)
        one16 = sb("one16", [128, 1], f16)
        onebf = sb("onebf", [128, 1], bf16)
        minus_half = sb("minus_half", [128, 8], f32)
        peak = sb("peak", [128, 8], f32)
        total = sb("total", [128, 8], f32)
        inverse = sb("inverse", [128, 8], f32)
        q_ms = sb("q_ms", [128, 8], f32)
        q_rms = sb("q_rms", [128, DEEP, 8], f32)
        k_ms = sb("k_ms", [128, XKV], f32)
        k_rms = sb("k_rms", [128, XKV], f32)
        stats = sb("stats", [128, 2, 6], f32)
        moments = sb("moments", [128, 2, 2], f32)
        ln_var = sb("ln_var", [128, 2], f32)
        ln_rstd = sb("ln_rstd", [128, 2], f32)
        gather = ctx.enter_context(nc.psum_tensor("gather", [128, 512], f32))
        banks = [ctx.enter_context(nc.psum_tensor(f"bank{i}", [128, 512], f32)) for i in range(NBANK)]

        w_qkv = w_a[:, 0:3072].rearrange("p (l k n) -> p l k n", l=2, k=KC)
        w_aout = w_a[:, 3072:4096].rearrange("p (l k n) -> p l k n", l=2, k=KC)
        w_down = w_a[:, :].rearrange("p (e l f n) -> p e l f n", e=2, l=2, f=FC)
        w_up = w_kv[:, :, :, :].rearrange("p e l (k n) -> p e l k n", k=KC)
        w_xq_v = w_xq[:, :, :, :].rearrange("p g l (k n) -> p g l k n", k=KC)
        w_xo_v = w_xo[:, :, :, :].rearrange("p g l (h n) -> p g l h n", h=GH)
        ctx_parts = parts[:, :, :].rearrange("p s (l k n) -> p s l k n", l=2, k=KC)
        hid_room = parts, w_xq[:, 0, :, :]
        hid_parts = [a[:, :, :].rearrange("p l (f n) -> p l f n", f=FC) for a in hid_room]
        attn_x = attn[:, :, :].rearrange("p l (h n) -> p l h n", h=GH)

        filled = sem("filled")
        freed = {"dve": sem("freed_by_dve"), "act": sem("freed_by_act")}
        s_const = sem("s_const")
        s_const_late = sem("s_const_late")
        s_cols = sem("s_cols")
        s_rows_in = sem("s_rows_in")
        s_resid = [sem(f"s_resid{t}") for t in range(NT)]
        s_staged = [sem(f"s_staged{i}") for i in range(NSTAGE + NEARLY)]
        s_high = sem("s_high")
        s_low = {False: sem("s_low_dve"), True: sem("s_low_pool")}
        s_zero = sem("s_zero")
        s_spread_zero = sem("s_spread_zero")
        s_made = sem("s_made")
        s_rows = sem("s_rows")
        s_aq_hi, s_ak_hi, s_av_hi = sem("s_aq_hi"), sem("s_ak_hi"), sem("s_av_hi")
        s_v_hi, s_key_hi, s_attn_hi, s_acts_hi = sem("s_v_hi"), sem("s_key_hi"), sem("s_attn_hi"), sem("s_acts_hi")
        s_q_hi = sem("s_q_hi")
        s_av_copied, s_v_copied = sem("s_av_copied"), sem("s_v_copied")
        s_k_read = sem("s_k_read")
        s_k_sum, s_k_ms, s_k_rms, s_k_normed = sem("s_k_sum"), sem("s_k_ms"), sem("s_k_rms"), sem("s_k_normed")
        s_masked, s_peak, s_shifted, s_exp = sem("s_masked"), sem("s_peak"), sem("s_shifted"), sem("s_exp")
        s_total, s_inverse, s_prob = sem("s_total"), sem("s_inverse"), sem("s_prob")
        s_prob_hi, s_probs = sem("s_prob_hi"), sem("s_probs")
        s_values = sem("s_values")
        s_even_values = sem("s_even_values")
        s_gather_read = sem("s_gather_read")
        s_sq_hi, s_sq = sem("s_sq_hi"), sem("s_sq")
        s_q_ms, s_q_rms = sem("s_q_ms"), sem("s_q_rms")
        s_stats, s_moments, s_var, s_rstd, s_normed = (
            sem("s_stats"), sem("s_moments"), sem("s_var"), sem("s_rstd"), sem("s_normed"))
        s_logits, s_route0, s_route = sem("s_logits"), sem("s_route0"), sem("s_route")
        s_hid_hi, s_hid = sem("s_hid_hi"), sem("s_hid")
        s_stored = sem("s_stored")

        block = ctx.enter_context(nc.Block())

        def bank_of(job):
            return banks[job % NBANK]

        def job_of(name, k, i=0):
            return FIRST_JOB[name, k] + i

        def wait_filled(eng, job):
            eng.wait_ge(filled, job + 1)

        def wait_bank(eng, job):
            if job >= NBANK:
                engine, count = JOB_ENDS[job - NBANK]
                eng.wait_ge(freed[engine], count)

        def wait_read(eng, job):
            engine, count = JOB_ENDS[job]
            eng.wait_ge(freed[engine], count)

        def wait_item(eng, kind, k=0):
            i = ITEMS.index((kind, k))
            on_pool = LOW_ON_POOL[i]
            eng.wait_ge(s_low[on_pool], sum(LOW_ON_POOL[j] == on_pool for j in range(i + 1)))

        NORMS, TURNS, UPS = keys_of("norm", "dve"), keys_of("norm_turn", "act"), keys_of("f_up", "act")

        def norm_no(k):
            return NORMS.index(k)

        def item_parts(i):
            kind, k = ITEMS[i]
            if kind == "x":
                return [acts[:, l, :, k * T:(k + 1) * T] for l in range(2)]
            if kind == "qk":
                return [w_qkv[:, l, :, 0:512] for l in range(2)]
            if kind == "v":
                return [w_qkv[:, l, :, 512:768] for l in range(2)]
            if kind == "ctx":
                return [ctx_parts[:, k % 2, l, :, :] for l in range(2)]
            if kind in ("wk", "wv"):
                return [w_up[:, int(kind == "wv"), l, :, :] for l in range(2)]
            if kind == "aout":
                return [w_aout[:, l, :, :] for l in range(2)]
            if kind == "xq":
                return [w_xq_v[:, k % 2, l, :, :] for l in range(2)]
            if kind == "xo":
                return [w_xo_v[:, k % 2, l, :, :] for l in range(2)]
            if kind == "up":
                return [w_up[:, k, l, :, :] for l in range(2)]
            return [w_down[:, k, l, :, :] for l in range(2)]

        def item_source(i):
            kind, k = ITEMS[i]
            by_chunk = lambda a: a.rearrange("(k p) n -> p k n", p=128)
            if kind == "x":
                return by_chunk(xT)[:, :, k * T:(k + 1) * T]
            if kind == "ctx":
                return by_chunk(ctxT)[:, :, k * T:(k + 1) * T]
            if kind == "qk":
                return by_chunk(wqkvT)[:, :, 0:512]
            if kind == "v":
                return by_chunk(wqkvT)[:, :, 512:768]
            if kind == "xq":
                return by_chunk(Wq)[:, :, k * 512:(k + 1) * 512]
            if kind == "xo":
                return by_chunk(Wo)[:, k * GH:(k + 1) * GH, :]
            return by_chunk({"wk": Wk, "wv": Wv, "aout": woutT, "up": WupT[k], "down": WdownT[k]}[kind])

        def slot_of(i):
            if i < NEARLY:
                return NSTAGE + i, 0
            return (i - NEARLY) % NSTAGE, (i - NEARLY) // NSTAGE

        def item_stage(i):
            shape, slot = item_source(i).shape, slot_of(i)[0]
            if slot < NSTAGE:
                at = stage[:, slot, 0:shape[1] * shape[2]]
            else:
                early = slot - NSTAGE
                at = values_hi[:, 4 * early:4 * early + 4, :].rearrange("p b n -> p (b n)")\
                    .bitcast(f32)[:, 0:shape[1] * shape[2]]
            return at.rearrange("p (k n) -> p k n", k=shape[1])

        def wait_split(eng, i):
            on_pool = LOW_ON_POOL[i]
            eng.wait_ge(s_low[on_pool], sum(LOW_ON_POOL[j] == on_pool for j in range(i + 1)))

        def wait_item_room(eng, i):
            kind, k = ITEMS[i]
            if kind == "ctx" and k >= 2:
                wait_filled(eng, job_of("v_project", 2 * (k - 2) + 1))
            if kind == "xq" and k >= 2:
                wait_filled(eng, job_of("x_query", (k - 2) * NT + NT - 1, 1))
            if kind == "xo" and k >= 2:
                wait_filled(eng, job_of("x_out", (k - 2) * NT + NT - 1))
            if kind == "up":
                wait_filled(eng, job_of("v_project", NC - 1))
            if kind == "down":
                wait_filled(eng, job_of("a_out", NT - 1))

        def wait_unit_used(eng, n):
            if n >= NA:
                wait_filled(eng, job_of("x_values", n - NA, 1))
            else:
                eng.wait_ge(s_values, n + 1)

        def resid_of(t):
            return resid[:, 2 * t:2 * t + 2, :].rearrange("p j n -> p (j n)")

        def blocks(ap):
            return ap.rearrange("p (k n) -> p k n", n=S)

        def query_slots(ap, h):
            pair = ap[:, h // 2 * 512:(h // 2 + 1) * 512].rearrange("p (b n) -> p b n", b=4)
            return pair[:, :, h % 2 * S:(h % 2 + 1) * S]

        def each_block(ap):
            return ap.unsqueeze(2).to_broadcast([128, 8, S])

        def all_blocks(ap):
            return ap.unsqueeze(1).to_broadcast([128, 8, S])

        def prob_part(n, low, parity):
            at = S if low != bool(parity) else 0
            return probs[:, n % DEEP, 4 * parity:4 * parity + 4, at:at + S]

        @block.sync
        def _(sp):
            for name, k in ORDER["sp"]:
                if name == "load":
                    i = k
                    if i >= NEARLY + NSTAGE:
                        wait_split(sp, i - NSTAGE)
                    sp.dma_start(item_stage(i), item_source(i)).then_inc(s_staged[slot_of(i)[0]], 16)
                    if i == 1:
                        sp.wait_ge(s_zero, 1)
                        for part in range(2):
                            sp.dma_start(scores[part:part + 97:32, 0:2, :].rearrange("p a n -> p (a n)")[:, 0:RW],
                                         bias_rows).then_inc(s_rows_in, 16)
                        sp.dma_start(cols[:, :], columns).then_inc(s_cols, 16)
                    if i == NEARLY - 1:
                        for dst, src in ((ident[:, :], identity), (causal_sb[0:64, :], causal),
                                         (causal_sb[64:128, :], causal)):
                            sp.dma_start(dst, src).then_inc(s_const, 16)
                    if i == NEARLY + NSTAGE - 1:
                        for dst, src in ((mask_sb[0:64, :], mask), (mask_sb[64:128, :], mask),
                                         (gate_sb[:, :, :], gate_w.partition_broadcast(128))):
                            sp.dma_start(dst, src).then_inc(s_const_late, 16)
                        for t in range(NT):
                            sp.dma_start(resid[:, 2 * t:2 * t + 2, :],
                                         x[t * T:(t + 1) * T, :].rearrange("(j p) n -> p j n", p=128))\
                                .then_inc(s_resid[t], 16)

                elif name == "v_copies":
                    sp.wait_ge(s_av_hi, 2 * (k + 1))
                    sp.wait_ge(s_spread_zero, 1)
                    if k:
                        wait_unit_used(sp, 4 * k - 1)
                    for j in range(2):
                        for b, lo, hi in ((2 * j, 0, 64), (2 * j + 1, 64, 128)):
                            other = slice(64 - lo, 128 - lo)
                            sp.dma_start(a_values_hi[lo:hi, b, :], v_spread[lo:hi, j, :])\
                                .then_inc(s_av_copied, 16)
                            sp.dma_start(a_values_hi[other, b, :], v_spread[lo:hi, j, :])\
                                .then_inc(s_av_copied, 16)

                elif name == "kv_copies":
                    sp.wait_ge(s_v_hi, k + 1)
                    wait_split(sp, k // 2)
                    for b, lo, hi in ((2 * k, 0, 64), (2 * k + 1, 64, 128)):
                        other = slice(64 - lo, 128 - lo)
                        sp.dma_start(values_hi[lo:hi, b, :], v_parts[lo:hi, :]).then_inc(s_v_copied, 16)
                        sp.dma_start(values_hi[other, b, :], v_parts[lo:hi, :]).then_inc(s_v_copied, 16)

                elif name == "store":
                    sp.wait_ge(s_normed, norm_no((2, k)) + 1)
                    sp.dma_start(out[k * T:(k + 1) * T, :].rearrange("(j p) n -> p j n", p=128),
                                 resid[:, 2 * k:2 * k + 2, :]).then_inc(s_stored, 16)
            sp.wait_ge(s_stored, 16 * NT)

        @block.scalar
        def _(act):
            for name, k in ORDER["act"]:
                if name == "load":
                    act.wait_ge(s_staged[slot_of(k)[0]], 16 * (slot_of(k)[1] + 1))
                    wait_item_room(act, k)
                    act.activation(item_parts(k)[0], item_stage(k), ACT.Copy).then_inc(s_high, 1)

                elif name == "a_read":
                    job = job_of("a_project", k)
                    wait_filled(act, job)
                    act.wait_ge(s_cols, 16)
                    if k:
                        wait_filled(act, job_of("a_scores", 4 * k - 1))
                    for e in range(2):
                        act.activation(a_q[:, 0, :, e * S:(e + 1) * S], blocks(bank_of(job)[:, :]), ACT.Copy,
                                       scale=cols[:, C_HEAD + e:C_HEAD + e + 1]).then_inc(s_aq_hi, 1)
                    wait_filled(act, job + 1)
                    act.activation(a_k[:, 0, :], bank_of(job + 1)[:, :], ACT.Copy).then_inc(s_ak_hi, 1)
                    wait_filled(act, job + 2)
                    act.wait_ge(s_spread_zero, 1)
                    if k:
                        act.wait_ge(s_av_copied, 16 * 8 * k)
                    bank = bank_of(job + 2)[:, :].rearrange("p (j i n) -> p j i n", j=2, n=2 * SD)
                    for e in range(2):
                        spread = v_spread[:, :, :].rearrange("p j (i n) -> p j i n", n=4 * SD)
                        act.activation(spread[:, :, :, 3 * SD * e:3 * SD * e + SD],
                                       bank[:, :, :, SD * e:SD * e + SD], ACT.Copy).then_inc(s_av_hi, 1)

                elif name == "k_read":
                    job = job_of("k_project", k)
                    wait_filled(act, job)
                    if k:
                        act.wait_ge(s_k_sum, k)
                    act.activation(k_sq[:, :], bank_of(job)[:, :], ACT.Square).then_inc(s_k_read, 1)
                    if k:
                        wait_filled(act, job_of("k_turn", k - 1))
                    act.activation(k_raw[:, :], bank_of(job)[:, :], ACT.Copy).then_inc(freed["act"], 1)

                elif name == "v_read":
                    job = job_of("v_project", k)
                    wait_filled(act, job)
                    if k:
                        act.wait_ge(s_v_copied, 16 * 4 * k)
                    act.activation(v_parts[:, :], bank_of(job)[:, :], ACT.Copy).then_inc(s_v_hi, 1)

                elif name == "k_turn_read":
                    job = job_of("k_turn", k)
                    wait_filled(act, job)
                    act.wait_ge(s_made, 7)
                    act.activation(keys[:, 0, :, k * 128:(k + 1) * 128],
                                   bank_of(job)[:, :].rearrange("p (g n) -> p g n", g=XKV), ACT.Copy,
                                   scale=key_scale[:, 0:1]).then_inc(s_key_hi, 1)

                elif name == "soft_exp":
                    act.wait_ge(s_shifted, k + 1)
                    act.activation(scores[:, k % DEEP, :], scores[:, k % DEEP, :], ACT.Exp).then_inc(s_exp, 1)

                elif name == "soft_hi":
                    act.wait_ge(s_prob, k + 1)
                    if k >= DEEP:
                        wait_filled(act, job_of("turn", k - DEEP))
                    for parity in range(2):
                        act.activation(prob_part(k, False, parity),
                                       blocks(scores[:, k % DEEP, :])[:, 4 * parity:4 * parity + 4, :],
                                       ACT.Copy).then_inc(s_prob_hi, 1)

                elif name == "turn_read":
                    job = job_of("turn", k)
                    wait_filled(act, job)
                    if k >= DEEP:
                        wait_unit_used(act, k - DEEP)
                    turned = act.activation(probsT[:, k % DEEP, :, :].rearrange("p k n -> p (k n)"),
                                            bank_of(job)[:, :].bitcast(f16), ACT.Copy)
                    turned.then_inc(freed["act"], 1)

                elif name == "a_split":
                    wait_unit_used(act, 4 * k + 3)
                    if k:
                        wait_filled(act, job_of("a_out", k - 1))
                    act.activation(attn[:, 0, 0:512], gather[:, :], ACT.Copy)\
                        .then_inc(s_attn_hi, 1)

                elif name == "norm_turn":
                    job = job_of(name, k)
                    wait_filled(act, job)
                    act.activation(acts[:, 0, :, k[1] * T:(k[1] + 1) * T],
                                   bank_of(job)[:, :].rearrange("p (k n) -> p k n", k=KC), ACT.Copy)\
                        .then_inc(s_acts_hi, 1)

                elif name == "q_parts":
                    u, pair = k
                    g, job = u // NT, job_of("x_query", u, pair)
                    if k == (0, 0):
                        wait_filled(act, job_of("a_scores", NA - 1))
                    if k == (1, 0):
                        wait_unit_used(act, NA - 1)
                    if u >= DEEP and pair == 0:
                        wait_filled(act, job_of("x_scores", u - DEEP))
                    wait_filled(act, job)
                    if u >= 2 and pair == 0:
                        act.wait_ge(s_sq, u - 1)
                    for e in range(2):
                        h = 2 * pair + e
                        bias = cols[:, C_BQ + GH * g + h:C_BQ + GH * g + h + 1]
                        head = blocks(bank_of(job)[:, e * T:(e + 1) * T])
                        act.activation(query_slots(queries[:, u % DEEP, 0, :], h), head, ACT.Identity,
                                       bias=bias).then_inc(s_q_hi, 1)
                        act.activation(query_slots(sq[u % 2], h), head, ACT.Square, bias=bias).then_inc(s_q_hi, 1)

                elif name == "sq_parts":
                    act.wait_ge(s_q_hi, 8 * (k + 1))
                    if k:
                        wait_filled(act, job_of("x_squares", k - 1))
                    act.activation(sq_hi, sq[k % 2], ACT.Copy).then_inc(s_sq_hi, 1)

                elif name == "x_values_read":
                    u, parity = k
                    job = job_of("x_values", u, parity)
                    wait_filled(act, job)
                    if parity == 0:
                        wait_filled(act, job_of("x_out", u - 1) if u else job_of("a_out", NT - 1))
                    act.activation(
                        attn_x[:, 0, :, :].rearrange("p h (c r q) -> p r c h q", r=2, q=S)[:, parity],
                        bank_of(job)[:, :].rearrange("p (c h q) -> p c h q", h=GH, q=S), ACT.Copy)\
                        .then_inc(s_attn_hi, 1)

                elif name == "f_up":
                    t, e, f = k
                    job, n = job_of(name, k), UPS.index(k)
                    wait_filled(act, job)
                    if n >= 2:
                        act.wait_ge(s_hid, n - 1)
                    else:
                        wait_filled(act, job_of("k_turn", NC - 1))
                    for i in range(2):
                        c = C_BUP + FC * e + 2 * f + i
                        done = act.activation(hidden[n % 2][:, i * T:(i + 1) * T],
                                              bank_of(job)[:, i * T:(i + 1) * T],
                                              ACT.Relu if e else ACT.Gelu, bias=cols[:, c:c + 1])
                    done.then_inc(freed["act"], 1)

        @block.vector
        def _(dve):
            dve.memset(scores[:, :, :], 0.0).then_inc(s_zero, 1)
            dve.memset(ones[:, :].bitcast(f32), 1.0).then_inc(s_made, 1)
            dve.memset(minus_half[:, :], -0.5).then_inc(s_made, 1)
            dve.memset(one16[:, :], 1.0).then_inc(s_made, 1)
            dve.memset(onebf[:, :], 1.0).then_inc(s_made, 1)
            dve.wait_ge(s_rows_in, 32)
            dve.wait_ge(s_cols, 16)
            raw = scores[:, :, :].rearrange("p a n -> p (a n)")[:, 0:RW]
            rounded = w_xq[:, 1, 1, 0:RW]
            dve.tensor_copy(rounded, raw).then_inc(s_rows, 1)
            dve.wait_ge(s_rows, 1)
            dve.scalar_tensor_tensor(rows[:, :], rounded.bitcast(f32), cols[:, C_SECOND:C_SECOND + 1], raw,
                                     ALU.mult, ALU.add).then_inc(s_rows, 1)

            for name, k in ORDER["dve"]:
                if name == "constants":
                    dve.wait_ge(s_const, 16 * 3)
                    dve.wait_ge(s_cols, 16)
                    dve.tensor_copy(ident16[:, :], ident[:, :]).then_inc(s_made, 1)
                    dve.tensor_tensor(key_scale[:, :], cols[:, C_QN:C_QN + 1], cols[:, C_KN:C_KN + 1], ALU.mult)\
                        .then_inc(s_made, 1)
                    dve.wait_ge(s_made, 6)
                    dve.tensor_scalar(key_scale[:, :], key_scale[:, :], float(XD) ** -0.5, None, ALU.mult)\
                        .then_inc(s_made, 1)

                elif name == "load":
                    if not LOW_ON_POOL[k]:
                        dve.wait_ge(s_high, k + 1)
                        dve.tensor_tensor(item_parts(k)[1], item_stage(k), item_parts(k)[0].bitcast(f32),
                                          ALU.subtract).then_inc(s_low[False], 1)

                elif name == "a_read":
                    job = job_of("a_project", k)
                    dve.wait_ge(s_aq_hi, 2 * (k + 1))
                    for e in range(2):
                        done = dve.scalar_tensor_tensor(
                            a_q[:, 1, :, e * S:(e + 1) * S], blocks(bank_of(job)[:, :]),
                            cols[:, C_HEAD + e:C_HEAD + e + 1], a_q[:, 0, :, e * S:(e + 1) * S],
                            ALU.mult, ALU.subtract)
                    done.then_inc(freed["dve"], 1)
                    dve.wait_ge(s_ak_hi, k + 1)
                    dve.tensor_tensor(a_k[:, 1, :], bank_of(job + 1)[:, :], a_k[:, 0, :], ALU.subtract)\
                        .then_inc(freed["dve"], 1)
                    dve.wait_ge(s_av_hi, 2 * (k + 1))
                    bank = bank_of(job + 2)[:, :].rearrange("p (j i n) -> p j i n", j=2, n=2 * SD)
                    spread, low = (a.rearrange("p j (i n) -> p j i n", n=4 * SD)
                                   for a in (v_spread[:, :, :], a_values_lo[:, k % 2, :, :]))
                    if k >= 2:
                        wait_unit_used(dve, 4 * (k - 1) - 1)
                    else:
                        dve.wait_ge(s_spread_zero, 2)
                    for e in range(2):
                        to = slice(3 * SD * e, 3 * SD * e + SD)
                        done = dve.tensor_tensor(low[:, :, :, to], bank[:, :, :, SD * e:SD * e + SD],
                                                 spread[:, :, :, to], ALU.subtract)
                    done.then_inc(freed["dve"], 1)

                elif name == "k_read":
                    dve.wait_ge(s_k_read, k + 1)
                    if k:
                        dve.wait_ge(s_k_rms, k)
                    dve.tensor_reduce(k_ms[:, :], k_sq[:, :].rearrange("p (g n) -> p g n", g=XKV), AX.X,
                                      ALU.add).then_inc(s_k_sum, 1)
                    dve.wait_ge(s_k_sum, k + 1)
                    dve.tensor_scalar(k_ms[:, :], k_ms[:, :], 1.0 / XD, RMS_EPS, ALU.mult, ALU.add)\
                        .then_inc(s_k_ms, 1)

                elif name == "v_read":
                    dve.wait_ge(s_v_hi, k + 1)
                    dve.tensor_tensor(values_lo[:, k, :], bank_of(job_of("v_project", k))[:, :], v_parts[:, :],
                                      ALU.subtract).then_inc(freed["dve"], 1)

                elif name == "k_turn_read":
                    dve.wait_ge(s_key_hi, k + 1)
                    at = slice(k * 128, (k + 1) * 128)
                    dve.scalar_tensor_tensor(
                        keys[:, 1, :, at], bank_of(job_of("k_turn", k))[:, :].rearrange("p (g n) -> p g n", g=XKV),
                        key_scale[:, 0:1], keys[:, 0, :, at], ALU.mult, ALU.subtract).then_inc(freed["dve"], 1)

                elif name == "soft_a":
                    if k >= DEEP:
                        dve.wait_ge(s_probs, k - DEEP + 1)
                    if k < NA:
                        job = job_of("a_scores", k)
                        wait_filled(dve, job)
                        dve.scalar_tensor_tensor(blocks(scores[:, k % DEEP, :]), blocks(bank_of(job)[:, :]),
                                                 float(SD) ** -0.5, all_blocks(causal_sb[:, :]),
                                                 ALU.mult, ALU.add).then_inc(freed["dve"], 1)
                    else:
                        u = k - NA
                        job = job_of("x_scores", u)
                        wait_filled(dve, job)
                        dve.wait_ge(s_q_rms, u + 1)
                        dve.tensor_tensor(blocks(scores[:, k % DEEP, :]), blocks(bank_of(job)[:, :]),
                                          each_block(q_rms[:, u % DEEP, :]), ALU.mult).then_inc(freed["dve"], 1)

                elif name == "soft_m":
                    if k < NA:
                        wait_read(dve, job_of("a_scores", k))
                    else:
                        dve.wait_ge(s_masked, k - NA + 1)
                    if k:
                        dve.wait_ge(s_shifted, k)
                    dve.tensor_reduce(peak[:, :], blocks(scores[:, k % DEEP, :]), AX.X, ALU.max)\
                        .then_inc(s_peak, 1)

                elif name == "soft_b":
                    dve.wait_ge(s_exp, k + 1)
                    dve.tensor_reduce(total[:, :], blocks(scores[:, k % DEEP, :]), AX.X, ALU.add)\
                        .then_inc(s_total, 1)
                    dve.wait_ge(s_total, k + 1)
                    if k:
                        dve.wait_ge(s_prob, k)
                    dve.reciprocal(inverse[:, :], total[:, :]).then_inc(s_inverse, 1)

                elif name == "soft_c":
                    dve.wait_ge(s_prob_hi, 2 * (k + 1))
                    for parity in range(2):
                        done = dve.tensor_tensor(
                            prob_part(k, True, parity),
                            blocks(scores[:, k % DEEP, :])[:, 4 * parity:4 * parity + 4, :],
                            prob_part(k, False, parity), ALU.subtract)
                    done.then_inc(s_probs, 1)

                elif name == "a_split":
                    dve.wait_ge(s_attn_hi, k + 1)
                    dve.tensor_tensor(attn[:, 1, 0:512], gather[:, :], attn[:, 0, 0:512].bitcast(f32),
                                      ALU.subtract).then_inc(s_gather_read, 1)

                elif name == "a_out":
                    job = job_of(name, k)
                    wait_filled(dve, job)
                    dve.wait_ge(s_resid[k], 16)
                    dve.tensor_tensor(resid_of(k), bank_of(job)[:, :], resid_of(k), ALU.add)\
                        .then_inc(freed["dve"], 1)

                elif name == "norm":
                    w, t = k
                    wait_read(dve, (job_of("a_out", t), job_of("x_out", NX - NT + t) if w else 0,
                                    job_of("f_down", (t, 1)) if w else 0)[w])
                    n = norm_no(k)
                    if n:
                        dve.wait_ge(s_normed, n)
                    for j in range(2):
                        dve.bn_stats(stats[:, j, :], resid[:, 2 * t + j, :]).then_inc(s_stats, 1)
                    dve.wait_ge(s_stats, 2 * n + 2)
                    for j in range(2):
                        dve.bn_aggr(moments[:, j, :], stats[:, j, :]).then_inc(s_moments, 1)
                    dve.wait_ge(s_moments, 2 * n + 2)
                    dve.tensor_scalar(ln_var[:, :], moments[:, :, 1], LN_EPS, None, ALU.add).then_inc(s_var, 1)

                elif name == "norm_end":
                    t = k[1]
                    dve.wait_ge(s_rstd, norm_no(k) + 1)
                    for j in range(2):
                        done = dve.tensor_scalar(resid[:, 2 * t + j, :], resid[:, 2 * t + j, :],
                                                 moments[:, j, 0:1], ln_rstd[:, j:j + 1],
                                                 ALU.subtract, ALU.mult)
                    done.then_inc(s_normed, 1)

                elif name == "norm_turn":
                    wait_high = TURNS.index(k) + 1
                    dve.wait_ge(s_acts_hi, wait_high)
                    at = slice(k[1] * T, (k[1] + 1) * T)
                    dve.tensor_tensor(acts[:, 1, :, at],
                                      bank_of(job_of(name, k))[:, :].rearrange("p (k n) -> p k n", k=KC),
                                      acts[:, 0, :, at].bitcast(f32), ALU.subtract).then_inc(freed["dve"], 1)

                elif name == "q_parts":
                    u, pair = k
                    g, job = u // NT, job_of("x_query", u, pair)
                    dve.wait_ge(s_q_hi, 8 * u + 4 * pair + 4)
                    for e in range(2):
                        h = 2 * pair + e
                        done = dve.scalar_tensor_tensor(
                            query_slots(queries[:, u % DEEP, 1, :], h), blocks(bank_of(job)[:, e * T:(e + 1) * T]),
                            cols[:, C_BQ + GH * g + h:C_BQ + GH * g + h + 1],
                            query_slots(queries[:, u % DEEP, 0, :], h), ALU.add, ALU.subtract)
                    done.then_inc(freed["dve"], 1)

                elif name == "x_squares":
                    job = job_of(name, k)
                    wait_filled(dve, job)
                    if k:
                        dve.wait_ge(s_q_rms, k)
                    dve.tensor_scalar(q_ms[:, :], bank_of(job)[:, 0:8], 1.0 / XD, RMS_EPS, ALU.mult, ALU.add)\
                        .then_inc(freed["dve"], 1)

                elif name == "x_values_read":
                    u, parity = k
                    dve.wait_ge(s_attn_hi, NT + 2 * u + parity + 1)
                    at = lambda l: attn_x[:, l, :, :].rearrange(
                        "p h (c r q) -> p r c h q", r=2, q=S)[:, parity]
                    dve.tensor_tensor(
                        at(1), bank_of(job_of("x_values", u, parity))[:, :].rearrange(
                            "p (c h q) -> p c h q", h=GH, q=S),
                        at(0).bitcast(f32), ALU.subtract).then_inc(freed["dve"], 1)

                elif name == "x_add":
                    t = k % NT
                    job = job_of("x_out", k)
                    wait_filled(dve, job)
                    if k < NT:
                        dve.wait_ge(s_normed, norm_no((0, t)) + 1)
                    else:
                        wait_read(dve, job_of("x_out", k - NT))
                    dve.tensor_tensor(resid_of(t), bank_of(job)[:, :], resid_of(t), ALU.add)\
                        .then_inc(freed["dve"], 1)

                elif name == "gate":
                    dve.wait_ge(s_sq, NX)
                    dve.wait_ge(s_const_late, 16 * 3)
                    dve.wait_ge(s_normed, norm_no((1, k)) + 1)
                    for j in range(2):
                        for e in range(2):
                            dve.tensor_tensor_reduce(gate_junk[:, :], resid[:, 2 * k + j, :], gate_sb[:, e, :],
                                                     1.0, 0.0, ALU.mult, ALU.add, logits[:, k, j, e:e + 1])\
                                .then_inc(s_logits, 1)
                            dve.wait_ge(s_logits, 4 * k + 2 * j + e + 1)
                    dve.tensor_tensor(routed[:, k, :, 0], logits[:, k, :, 0], logits[:, k, :, 1], ALU.is_ge)\
                        .then_inc(s_route0, 1)
                    dve.wait_ge(s_route0, k + 1)
                    dve.tensor_scalar(routed[:, k, :, 1], routed[:, k, :, 0], -1.0, 1.0, ALU.mult, ALU.add)\
                        .then_inc(s_route, 1)

                elif name == "f_up":
                    t, e, f = k
                    n = UPS.index(k)
                    dve.wait_ge(s_hid_hi, n + 1)
                    at = slice(f * 512, (f + 1) * 512)
                    dve.tensor_tensor(hid_room[e][:, 1, at], hidden[n % 2][:, :], hid_room[e][:, 0, at].bitcast(f32),
                                      ALU.subtract).then_inc(s_hid, 1)

                elif name == "f_down":
                    t, e = k
                    job = job_of(name, k)
                    wait_filled(dve, job)
                    dve.wait_ge(s_route, t + 1)
                    if e:
                        wait_read(dve, job_of(name, (t, 0)))
                    for j in range(2):
                        done = dve.scalar_tensor_tensor(resid[:, 2 * t + j, :], bank_of(job)[:, j * D:(j + 1) * D],
                                                        routed[:, t, j, e:e + 1], resid[:, 2 * t + j, :],
                                                        ALU.mult, ALU.add)
                    done.then_inc(freed["dve"], 1)

        @block.gpsimd
        def _(pool):
            pool.memset(v_spread[:, :, :], 0.0).then_inc(s_spread_zero, 1)
            pool.memset(a_values_lo[:, :, :, :], 0.0).then_inc(s_spread_zero, 1)
            for name, k in ORDER["pool"]:
                if name == "load":
                    if LOW_ON_POOL[k]:
                        pool.wait_ge(s_high, k + 1)
                        pool.tensor_tensor(item_parts(k)[1], item_stage(k), item_parts(k)[0].bitcast(f32),
                                           ALU.subtract).then_inc(s_low[True], 1)

                elif name == "k_read":
                    pool.wait_ge(s_k_ms, k + 1)
                    pool.wait_ge(s_made, 2)
                    pool.tensor_tensor(k_rms[:, :], k_ms[:, :], minus_half[:, 0:XKV], ALU.pow)\
                        .then_inc(s_k_rms, 1)
                    pool.wait_ge(s_k_rms, k + 1)
                    wait_read(pool, job_of("k_project", k))
                    by_head = k_raw[:, :].rearrange("p (g n) -> p g n", g=XKV)
                    pool.tensor_tensor(by_head, by_head, k_rms[:, :].unsqueeze(2).to_broadcast([128, XKV, XD]),
                                       ALU.mult).then_inc(s_k_normed, 1)

                elif name == "soft_mask":
                    pool.wait_ge(s_const_late, 16 * 3)
                    wait_read(pool, job_of("x_scores", k - NA))
                    at = blocks(scores[:, k % DEEP, :])
                    pool.tensor_tensor(at, at, all_blocks(mask_sb[:, :]), ALU.add).then_inc(s_masked, 1)

                elif name == "soft_shift":
                    pool.wait_ge(s_peak, k + 1)
                    at = blocks(scores[:, k % DEEP, :])
                    pool.tensor_tensor(at, at, each_block(peak[:, :]), ALU.subtract).then_inc(s_shifted, 1)

                elif name == "soft_scale":
                    pool.wait_ge(s_inverse, k + 1)
                    at = blocks(scores[:, k % DEEP, :])
                    pool.tensor_tensor(at, at, each_block(inverse[:, :]), ALU.mult).then_inc(s_prob, 1)

                elif name == "norm":
                    pool.wait_ge(s_var, norm_no(k) + 1)
                    pool.tensor_tensor(ln_rstd[:, :], ln_var[:, :], minus_half[:, 0:2], ALU.pow)\
                        .then_inc(s_rstd, 1)

                elif name == "sq_parts":
                    pool.wait_ge(s_sq_hi, k + 1)
                    if k == 0:
                        pool.wait_ge(s_av_copied, 16 * 8 * NT)
                    pool.tensor_tensor(sq_lo, sq[k % 2], sq_hi, ALU.subtract).then_inc(s_sq, 1)

                elif name == "q_pow":
                    wait_read(pool, job_of("x_squares", k))
                    if k >= DEEP:
                        wait_read(pool, job_of("x_scores", k - DEEP))
                    pool.tensor_tensor(q_rms[:, k % DEEP, :], q_ms[:, :], minus_half[:, :], ALU.pow)\
                        .then_inc(s_q_rms, 1)

                elif name == "f_up":
                    t, e, f = k
                    n = UPS.index(k)
                    wait_read(pool, job_of(name, k))
                    if t:
                        wait_filled(pool, job_of("f_down", (t - 1, e)))
                    elif e:
                        wait_filled(pool, job_of("x_query", NX - NT - 1, 1))
                    else:
                        wait_filled(pool, job_of("v_project", NC - 1))
                    pool.tensor_scalar(hid_room[e][:, 0, f * 512:(f + 1) * 512], hidden[n % 2][:, :], 1.0, 0.0,
                                       ALU.mult, ALU.add).then_inc(s_hid_hi, 1)

        @block.tensor
        def _(pe):
            def bias(out_ap, row, width, tokens_first, col=0):
                group, first = row
                at = slice(32 * group, 32 * group + 2)
                bias_row = rows[at, first + col:first + col + width]
                if tokens_first:
                    pe.matmul(out_ap, ones[at, 0:128], bias_row, start=True, stop=False)
                else:
                    pe.matmul(out_ap, bias_row, ones[at, 0:T], start=True, stop=False)

            half = slice(0, S), slice(S, 2 * S)

            def product(out_ap, still, moving, chunks, start):
                for c in range(chunks):
                    for i, (a, b) in enumerate(SPLITS):
                        done = pe.matmul(out_ap, still(a, c), moving(b, c), start=start and c == 0 and i == 0,
                                         stop=c == chunks - 1 and i == len(SPLITS) - 1)
                return done

            pe.wait_ge(s_made, 1)
            pe.wait_ge(s_rows, 2)
            for name, k in ORDER["pe"]:
                if name == "a_project":
                    wait_item(pe, "x", k)
                    wait_item(pe, "qk")
                    tile = slice(k * T, (k + 1) * T)
                    for which in range(2):
                        job = job_of(name, k, which)
                        wait_bank(pe, job)
                        for c in range(2):
                            to, col = bank_of(job)[:, c * T:(c + 1) * T], which * D + c * 128
                            bias(to, R_QKV, 128, False, col)
                            done = product(to, lambda l, q: w_qkv[:, l, q, col:col + 128],
                                           lambda l, q: acts[:, l, q, tile], KC, False)
                        done.then_inc(filled, 1)
                    wait_item(pe, "v")
                    job = job_of(name, k, 2)
                    wait_bank(pe, job)
                    for j in range(2):
                        to, tok = bank_of(job)[:, j * D:(j + 1) * D], k * T + j * 128
                        bias(to, R_QKV, D, True, 2 * D)
                        done = product(to, lambda l, q: acts[:, l, q, tok:tok + 128],
                                       lambda l, q: w_qkv[:, l, q, 2 * D:3 * D], KC, False)
                    done.then_inc(filled, 1)

                elif name == "a_scores":
                    job = job_of(name, k)
                    wait_read(pe, job_of("a_project", k // 4, 1))
                    wait_bank(pe, job)
                    rows32 = slice(32 * (k % 4), 32 * (k % 4) + 32)
                    for b in range(4):
                        for i in range(2):
                            tok = slice(i * T + b * S, i * T + (b + 1) * S)
                            at = block_of(b, i)
                            done = product(bank_of(job)[:, at * S:(at + 1) * S],
                                           lambda l, _: a_q[rows32, l, 4 * i + b, :],
                                           lambda l, _: a_k[rows32, l, tok], 1, True)
                    done.then_inc(filled, 1)

                elif name == "turn":
                    job = job_of(name, k)
                    pe.wait_ge(s_made, 7)
                    pe.wait_ge(s_probs, k + 1)
                    wait_bank(pe, job)
                    turned = bank_of(job)[:, :].bitcast(f16)
                    for at in range(8):
                        done = pe.transpose(turned[:, at * 128:(at + 1) * 128], probs[:, k % DEEP, at, :],
                                            ident16[:, :])
                    done.then_inc(filled, 1)

                elif name == "a_values":
                    t, r = k // 4, k % 4
                    wait_read(pe, job_of("turn", k))
                    if r == 0:
                        pe.wait_ge(s_av_copied, 16 * 8 * (t + 1))
                        if t:
                            pe.wait_ge(s_gather_read, t)
                    for parity in range(2):
                        if parity:
                            pe.wait_ge(s_even_values, k + 1)
                        for b in (parity, parity + 2):
                            for i in range(2):
                                to = gather[32 * r:32 * r + 32, i * T + b * S:i * T + (b + 1) * S]
                                for e in range(2):
                                    at = (4 * i + r) * 4 * SD + e * 2 * SD
                                    turned = probsT[:, k % DEEP, block_of(b, i), e * S:(e + 1) * S]
                                    pe.matmul(to, a_values_hi[:, b, at:at + 2 * SD], turned, start=e == 0,
                                              stop=False)
                                    done = pe.matmul(
                                        to, a_values_lo[half[parity], t % 2, b // 2, at:at + 2 * SD],
                                        turned[half[parity]], start=False, stop=e == 1)
                        done.then_inc((s_even_values, s_values)[parity], 1)

                elif name == "a_out":
                    job = job_of(name, k)
                    wait_item(pe, "aout")
                    pe.wait_ge(s_gather_read, k + 1)
                    wait_bank(pe, job)
                    for j in range(2):
                        to = bank_of(job)[:, j * D:(j + 1) * D]
                        bias(to, R_OUT, D, True)
                        done = product(to, lambda l, c: attn[:, l, c * T + j * 128:c * T + (j + 1) * 128],
                                       lambda l, c: w_aout[:, l, c, :], KC, False)
                    done.then_inc(filled, 1)

                elif name == "norm_turn":
                    job = job_of(name, k)
                    pe.wait_ge(s_normed, norm_no(k) + 1)
                    wait_bank(pe, job)
                    for c in range(KC):
                        for j in range(2):
                            done = pe.transpose(bank_of(job)[:, c * T + j * 128:c * T + (j + 1) * 128],
                                                resid[:, 2 * k[1] + j, c * 128:(c + 1) * 128], ident[:, :])
                    done.then_inc(filled, 1)

                elif name in ("k_project", "v_project"):
                    which = int(name == "v_project")
                    slot, at = (k // 2) % 2, slice((k % 2) * 128, (k % 2) * 128 + 128)
                    wait_item(pe, "ctx", k // 2)
                    job = job_of(name, k)
                    wait_item(pe, ("wk", "wv")[which])
                    wait_bank(pe, job)
                    bias(bank_of(job)[:, :], (R_K, R_V)[which], 512, True)
                    product(bank_of(job)[:, :], lambda l, c: ctx_parts[:, slot, l, c, at],
                            lambda l, c: w_up[:, which, l, c, :], KC, False).then_inc(filled, 1)

                elif name == "k_turn":
                    job = job_of(name, k)
                    pe.wait_ge(s_k_normed, k + 1)
                    wait_bank(pe, job)
                    for g in range(XKV):
                        done = pe.transpose(bank_of(job)[:, g * 128:(g + 1) * 128],
                                            k_raw[:, g * 128:(g + 1) * 128], ident[:, :])
                    done.then_inc(filled, 1)

                elif name == "x_query":
                    g, t = k // NT, k % NT
                    wait_item(pe, "xq", g)
                    wait_read(pe, job_of("norm_turn", (0, t)))
                    for pair in range(2):
                        job = job_of(name, k, pair)
                        wait_bank(pe, job)
                        for e in range(2):
                            h = 2 * pair + e
                            done = product(bank_of(job)[:, e * T:(e + 1) * T],
                                           lambda l, c: w_xq_v[:, g % 2, l, c, h * 128:(h + 1) * 128],
                                           lambda l, c: acts[:, l, c, t * T:(t + 1) * T], KC, True)
                        done.then_inc(filled, 1)

                elif name == "x_squares":
                    job = job_of(name, k)
                    pe.wait_ge(s_sq, k + 1)
                    wait_bank(pe, job)
                    for b in range(4):
                        for i in range(2):
                            at = block_of(b, i)
                            slot = slice((4 * i + b) * 128, (4 * i + b + 1) * 128)
                            pe.matmul(bank_of(job)[:, at:at + 1], sq_hi[:, slot], onebf[:, :],
                                      start=True, stop=False)
                            done = pe.matmul(bank_of(job)[:, at:at + 1], sq_lo[:, slot], one16[:, :],
                                             start=False, stop=True)
                    done.then_inc(filled, 1)

                elif name == "x_scores":
                    g, t = k // NT, k % NT
                    job = job_of(name, k)
                    wait_read(pe, job_of("x_query", k, 1))
                    wait_read(pe, job_of("k_turn", 2 * t + 1))
                    wait_bank(pe, job)
                    for b in range(4):
                        for i in range(2):
                            at, tok = block_of(b, i), (4 * t + b) * S
                            slot = slice((4 * i + b) * 128, (4 * i + b + 1) * 128)
                            done = product(bank_of(job)[:, at * S:(at + 1) * S],
                                           lambda l, _: queries[:, k % DEEP, l, slot],
                                           lambda l, _: keys[:, l, g, tok:tok + S], 1, True)
                    done.then_inc(filled, 1)

                elif name == "x_values":
                    g, t = k // NT, k % NT
                    wait_read(pe, job_of("turn", NA + k))
                    pe.wait_ge(s_v_copied, 16 * 4 * (2 * t + 2))
                    wait_read(pe, job_of("v_project", 2 * t + 1))
                    for parity in range(2):
                        job = job_of(name, k, parity)
                        wait_bank(pe, job)
                        for c in range(2):
                            b = 2 * c + parity
                            at = block_of(b, 0)
                            to, turned = bank_of(job)[:, c * T:(c + 1) * T], probsT[:, (NA + k) % DEEP, at:at + 2, :]
                            pe.matmul(to, values_hi[:, 4 * t + b, g * XD:(g + 1) * XD], turned,
                                      start=True, stop=False)
                            done = pe.matmul(to, values_lo[half[parity], 2 * t + c, g * XD:(g + 1) * XD],
                                             turned[half[parity]], start=False, stop=True)
                        done.then_inc(filled, 1)

                elif name == "x_out":
                    g, t = k // NT, k % NT
                    job = job_of(name, k)
                    wait_item(pe, "xo", g)
                    wait_read(pe, job_of("x_values", k, 1))
                    wait_bank(pe, job)
                    for j in range(2):
                        done = product(bank_of(job)[:, j * D:(j + 1) * D],
                                       lambda l, h: attn_x[:, l, h, j * 128:(j + 1) * 128],
                                       lambda l, h: w_xo_v[:, g % 2, l, h, :], GH, True)
                    done.then_inc(filled, 1)

                elif name == "f_up":
                    t, e, f = k
                    job = job_of(name, k)
                    wait_item(pe, "up", e)
                    wait_read(pe, job_of("norm_turn", (1, t)))
                    wait_bank(pe, job)
                    for i in range(2):
                        col = (2 * f + i) * 128
                        done = product(bank_of(job)[:, i * T:(i + 1) * T],
                                       lambda l, c: w_up[:, e, l, c, col:col + 128],
                                       lambda l, c: acts[:, l, c, t * T:(t + 1) * T], KC, True)
                    done.then_inc(filled, 1)

                elif name == "f_down":
                    t, e = k
                    job = job_of(name, k)
                    wait_item(pe, "down", e)
                    pe.wait_ge(s_hid, max(UPS.index((t, e, f)) for f in range(2)) + 1)
                    wait_bank(pe, job)
                    for j in range(2):
                        to = bank_of(job)[:, j * D:(j + 1) * D]
                        bias(to, R_DOWN[e], D, True)
                        done = product(to, lambda l, c: hid_parts[e][:, l, c, j * 128:(j + 1) * 128],
                                       lambda l, c: w_down[:, e, l, c, :], FC, False)
                    done.then_inc(filled, 1)


def kernel(x, ctx_2048, mask_1xSxS2_ff0, L0_attn_w_qkv, L0_attn_b_qkv, L0_attn_w_out, L0_attn_b_out,
           L0_xattn_Wq, L0_xattn_bq, L0_xattn_Wk, L0_xattn_bk, L0_xattn_Wv, L0_xattn_bv, L0_xattn_Wo,
           L0_xattn_qn_w, L0_xattn_kn_w, L0_ffn_Wg, L0_ffn_W0a, L0_ffn_b0a, L0_ffn_W0b, L0_ffn_b0b,
           L0_ffn_W1a, L0_ffn_b1a, L0_ffn_W1b, L0_ffn_b1b):
    import numpy as np
    import concourse.bacc as bacc
    from concourse.bass_utils import run_bass_kernel_spmd

    host = np.asarray
    b_qkv, b_out, bk, bv = host(L0_attn_b_qkv), host(L0_attn_b_out), host(L0_xattn_bk), host(L0_xattn_bv)
    b0b, b1b = host(L0_ffn_b0b), host(L0_ffn_b1b)
    f4 = np.float32
    row = np.arange(128)
    head = np.stack([(row // SD) % 2 == e for e in range(2)], 1).astype(f4)
    second = np.where(row % 32 == 1, -1.0, 0.0).astype(f4)[:, None]
    causal = np.where(np.arange(S)[None, :] <= np.arange(S)[:, None], 0.0, HIDDEN).astype(f4)
    arrays = {
        "xT": host(x).reshape(TOK, D).T, "x": host(x).reshape(TOK, D), "ctxT": host(ctx_2048).reshape(TOK, D).T,
        "wqkvT": host(L0_attn_w_qkv).T, "woutT": host(L0_attn_w_out).T, "Wq": host(L0_xattn_Wq),
        "Wk": host(L0_xattn_Wk), "Wv": host(L0_xattn_Wv), "Wo": host(L0_xattn_Wo),
        "WupT": np.stack([host(L0_ffn_W0a).T, host(L0_ffn_W1a).T]),
        "WdownT": np.stack([host(L0_ffn_W0b).T, host(L0_ffn_W1b).T]),
        "bias_rows": np.stack([b_qkv, np.concatenate([bk, b_out]), np.concatenate([bv, b0b]),
                               np.concatenate([b1b, b1b, b1b])]),
        "columns": np.concatenate([
            host(L0_xattn_bq).reshape(XH, XD).T, host(L0_ffn_b0a).reshape(FC, 128).T,
            host(L0_ffn_b1a).reshape(FC, 128).T, host(L0_xattn_qn_w)[:, None],
            host(L0_xattn_kn_w)[:, None], head, second], 1),
        "gate_w": host(L0_ffn_Wg), "mask": host(mask_1xSxS2_ff0)[0], "causal": causal,
        "identity": np.eye(128, dtype=f4),
    }
    nc = bacc.Bacc("TRN2", target_bir_lowering=False, num_devices=1)
    sent, args = {}, []
    for name, a in arrays.items():
        a = np.ascontiguousarray(a)
        sent[f"in_{name}"] = a
        args.append(nc.dram_tensor(f"in_{name}", a.shape, mybir.dt.from_np(a.dtype), kind="ExternalInput").ap())
    out = nc.dram_tensor("out", (TOK, D), mybir.dt.float32, kind="ExternalOutput").ap()
    decoder(nc, *args, out)
    result = run_bass_kernel_spmd(nc, [sent], core_ids=[0])
    return result.results[0]["out"].reshape(NB, S, D)
```
